# Optimizing a Trainium2 kernel written in Bass

```python
import numpy as np
import jax
import jax.numpy as jnp

def _softmax(x, axis=-1):
    return jax.nn.softmax(x, axis=axis)

def _gelu(x):
    return jax.nn.gelu(x, approximate=True)

def _silu(x):
    return jax.nn.silu(x)

def _sigmoid(x):
    return jax.nn.sigmoid(x)

def _layernorm(x, axis=-1, eps=1e-05):
    m = jnp.mean(x, axis=axis, keepdims=True)
    v = jnp.var(x, axis=axis, keepdims=True)
    return (x - m) / jnp.sqrt(v + eps)

def _scatter_add(tgt, idx, src, axis=0):
    return tgt.at[idx].add(src)

def _segment_sum(src, seg, n):
    return jax.ops.segment_sum(src, seg, n)
kernel_name = 'mk_xattn_ffn_d1_seqx_r4_e6dd6f'

def setup_inputs(seed: int=0):
    np.random.seed(seed)
    _w = jnp.asarray

    def _rec_inputs():
        import jax
        import jax.numpy as jnp
        _rk = jax.random.key(seed)
        x = 7.22e-05 + 1 * jax.random.normal(jax.random.fold_in(_rk, 1), (32, 128, 512), jnp.float32)
        _lenS = 128 - jax.random.randint(jax.random.fold_in(_rk, 7), (32,), 0, max(1, 128 // 4) + 1, jnp.int32)
        _lenS2 = 128 - jax.random.randint(jax.random.fold_in(_rk, 8), (32,), 0, max(1, 128 // 4) + 1, jnp.int32)
        _ctx_2048P = jax.random.normal(jax.random.fold_in(_rk, 12), (32, 16, 512), jnp.float32)
        _ctx_2048c = jax.random.dirichlet(jax.random.fold_in(_rk, 512), 0.3 * jnp.ones((16,), jnp.float32), (32, 128))
        _ctx_2048t = jnp.einsum('bsk,bkd->bsd', _ctx_2048c, _ctx_2048P)
        _ctx_2048t = _ctx_2048t * jax.lax.rsqrt(jnp.mean(jnp.square(_ctx_2048t)) + 1e-12) * 0.953939
        ctx_2048 = 0.00424091 + 1.0017 * (_ctx_2048t + 0.3 * jax.random.normal(jax.random.fold_in(_rk, 612), (32, 128, 512), jnp.float32))
        _validS = jnp.arange(128)[None, :] < _lenS[:, None]
        _validS2 = jnp.arange(128)[None, :] < _lenS2[:, None]
        _causal = jnp.tril(jnp.ones((128, 128), dtype=bool))
        mask_Bx1xSxS_fk0 = jnp.where(jnp.broadcast_to(_validS[:, None, None, :], (32, 1, 128, 128)), -1000000000.0, 0.0).astype(jnp.float32)
        return (x, ctx_2048, mask_Bx1xSxS_fk0)
    x, ctx_2048, mask_Bx1xSxS_fk0 = _rec_inputs()

    def _L0_xattn_setup():
        import jax, jax.numpy as jnp
        import numpy as np
        import math
        B, S, HID, H = (2, 512, 512, 32)
        D = HID // H
        AL = 10

        def _rope_tables(seq_len, dim, dtype):
            inv_freq = 1.0 / 10000.0 ** (np.arange(0, dim, 2, dtype=np.float32) / dim)
            t = np.arange(seq_len, dtype=np.float32)
            freqs = np.outer(t, inv_freq)
            emb = np.concatenate([freqs, freqs], -1)
            return (jnp.asarray(np.cos(emb), dtype), jnp.asarray(np.sin(emb), dtype))

        def _rotate_half(x):
            x1, x2 = jnp.split(x, 2, axis=-1)
            return jnp.concatenate([-x2, x1], axis=-1)
        key = jax.random.key(seed)
        ks = jax.random.split(key, 8)
        hidden_states = jax.random.normal(ks[0], (B, S, HID), dtype=jnp.float32)
        adapter = jax.random.normal(ks[1], (B, AL, HID), dtype=jnp.float32)
        causal = jnp.tril(jnp.ones((S, S), dtype=bool))
        attention_mask = jnp.broadcast_to(jnp.where(causal, 0.0, -1000000000.0).astype(jnp.float32)[None, None], (B, 1, S, S))
        scale = 0.02
        Wq = jax.random.normal(ks[2], (HID, HID), dtype=jnp.float32) * scale
        Wk = jax.random.normal(ks[3], (HID, HID), dtype=jnp.float32) * scale
        Wv = jax.random.normal(ks[4], (HID, HID), dtype=jnp.float32) * scale
        Wo = jax.random.normal(ks[5], (HID, HID), dtype=jnp.float32) * scale
        gate = jax.random.normal(ks[6], (1, H, 1, 1), dtype=jnp.float32) * 0.1
        return {'hidden_states': hidden_states, 'attention_mask': attention_mask, 'adapter': adapter, 'Wq': Wq, 'Wk': Wk, 'Wv': Wv, 'Wo': Wo, 'gate': gate}
    _L0_xattn_all = _L0_xattn_setup()
    _L0_xattn_in = {k: v for k, v in _L0_xattn_all.items() if k in ('Wq', 'Wk', 'Wv', 'Wo', 'gate')}
    del _L0_xattn_all

    def _L0_ffn_setup():
        import jax, jax.numpy as jnp
        import numpy as np
        H = 512
        I = 352
        E = 8
        K = 2
        B, S = (4, 512)

        def _moe(x, router_w, w1, w2):
            b, s, h = x.shape
            xf = x.reshape(-1, h)
            T = xf.shape[0]
            logits = xf @ router_w.T
            topk_vals, topk_idx = jax.lax.top_k(logits, K)
            topk_w = jax.nn.softmax(topk_vals, axis=-1)
            exp_id = topk_idx.reshape(-1)
            exp_w = topk_w.reshape(-1)
            order = jnp.argsort(exp_id)
            x_sorted = xf[order // K]
            counts = jnp.bincount(exp_id, length=E).astype(jnp.int32)
            y1 = jax.lax.ragged_dot(x_sorted, jnp.swapaxes(w1, 1, 2), counts)
            gate, up = jnp.split(y1, 2, axis=-1)
            y_act = jax.nn.silu(gate) * up
            y2 = jax.lax.ragged_dot(y_act, jnp.swapaxes(w2, 1, 2), counts)
            inv = jnp.argsort(order)
            y_pairs = y2[inv] * exp_w[:, None]
            y = y_pairs.reshape(T, K, h).sum(axis=1)
            return y.reshape(b, s, h)
        key = jax.random.key(seed)
        k1, k2, k3, k4 = jax.random.split(key, 4)
        x = jax.random.normal(k1, (B, S, H), dtype=jnp.float32)
        router_w = jax.random.normal(k2, (E, H), dtype=jnp.float32) * 0.02
        w1 = jax.random.normal(k3, (E, 2 * I, H), dtype=jnp.float32) * 0.02
        w2 = jax.random.normal(k4, (E, H, I), dtype=jnp.float32) * 0.02
        return {'x': x, 'router_w': router_w, 'w1': w1, 'w2': w2}
    _L0_ffn_all = _L0_ffn_setup()
    _L0_ffn_in = {k: v for k, v in _L0_ffn_all.items() if k in ('router_w', 'w1', 'w2')}
    del _L0_ffn_all
    return {'x': x, 'ctx_2048': ctx_2048, 'mask_Bx1xSxS_fk0': mask_Bx1xSxS_fk0, 'L0_xattn_Wq': _L0_xattn_in['Wq'], 'L0_xattn_Wk': _L0_xattn_in['Wk'], 'L0_xattn_Wv': _L0_xattn_in['Wv'], 'L0_xattn_Wo': _L0_xattn_in['Wo'], 'L0_xattn_gate': _L0_xattn_in['gate'], 'L0_ffn_router_w': _L0_ffn_in['router_w'], 'L0_ffn_w1': _L0_ffn_in['w1'], 'L0_ffn_w2': _L0_ffn_in['w2']}

def reference(x, ctx_2048, mask_Bx1xSxS_fk0, L0_xattn_Wq, L0_xattn_Wk, L0_xattn_Wv, L0_xattn_Wo, L0_xattn_gate, L0_ffn_router_w, L0_ffn_w1, L0_ffn_w2):
    import jax
    import jax.numpy as jnp

    def _L0_xattn_ref(hidden_states, attention_mask, adapter, Wq, Wk, Wv, Wo, gate):
        import jax, jax.numpy as jnp
        import numpy as np
        import math
        B, S, HID, H = (2, 512, 512, 32)
        D = HID // H
        AL = 10

        def _rope_tables(seq_len, dim, dtype):
            inv_freq = 1.0 / 10000.0 ** (np.arange(0, dim, 2, dtype=np.float32) / dim)
            t = np.arange(seq_len, dtype=np.float32)
            freqs = np.outer(t, inv_freq)
            emb = np.concatenate([freqs, freqs], -1)
            return (jnp.asarray(np.cos(emb), dtype), jnp.asarray(np.sin(emb), dtype))

        def _rotate_half(x):
            x1, x2 = jnp.split(x, 2, axis=-1)
            return jnp.concatenate([-x2, x1], axis=-1)
        bsz, q_len, hid = hidden_states.shape
        n_heads = gate.shape[1]
        head_dim = hid // n_heads
        inv_sqrt_d = 1.0 / math.sqrt(head_dim)

        def split_heads(x, length):
            return x.reshape(bsz, length, n_heads, head_dim).transpose(0, 2, 1, 3)
        q = split_heads(hidden_states @ Wq, q_len)
        k = split_heads(hidden_states @ Wk, q_len)
        v = split_heads(hidden_states @ Wv, q_len)
        cos, sin = _rope_tables(q_len, head_dim, q.dtype)
        q = q * cos + _rotate_half(q) * sin
        k = k * cos + _rotate_half(k) * sin
        scores = jnp.einsum('bhqd,bhkd->bhqk', q, k) * inv_sqrt_d
        scores = scores + attention_mask
        scores = jnp.maximum(scores, jnp.finfo(scores.dtype).min)
        w = jax.nn.softmax(scores.astype(jnp.float32), axis=-1).astype(q.dtype)
        attn_output = jnp.einsum('bhqk,bhkd->bhqd', w, v)
        adapter_len = adapter.shape[1]
        a_k = split_heads(adapter @ Wk, adapter_len)
        a_v = split_heads(adapter @ Wv, adapter_len)
        a_scores = jnp.einsum('bhqd,bhkd->bhqk', q, a_k) * inv_sqrt_d
        a_scores = jnp.tanh(gate) * jax.nn.softmax(a_scores.astype(jnp.float32), axis=-1).astype(q.dtype)
        attn_output = attn_output + jnp.einsum('bhqk,bhkd->bhqd', a_scores, a_v)
        attn_output = attn_output.transpose(0, 2, 1, 3).reshape(bsz, q_len, hid)
        return attn_output @ Wo

    def _L0_ffn_ref(x, router_w, w1, w2):
        import jax, jax.numpy as jnp
        import numpy as np
        H = 512
        I = 352
        E = 8
        K = 2
        B, S = (4, 512)

        def _moe(x, router_w, w1, w2):
            b, s, h = x.shape
            xf = x.reshape(-1, h)
            T = xf.shape[0]
            logits = xf @ router_w.T
            topk_vals, topk_idx = jax.lax.top_k(logits, K)
            topk_w = jax.nn.softmax(topk_vals, axis=-1)
            exp_id = topk_idx.reshape(-1)
            exp_w = topk_w.reshape(-1)
            order = jnp.argsort(exp_id)
            x_sorted = xf[order // K]
            counts = jnp.bincount(exp_id, length=E).astype(jnp.int32)
            y1 = jax.lax.ragged_dot(x_sorted, jnp.swapaxes(w1, 1, 2), counts)
            gate, up = jnp.split(y1, 2, axis=-1)
            y_act = jax.nn.silu(gate) * up
            y2 = jax.lax.ragged_dot(y_act, jnp.swapaxes(w2, 1, 2), counts)
            inv = jnp.argsort(order)
            y_pairs = y2[inv] * exp_w[:, None]
            y = y_pairs.reshape(T, K, h).sum(axis=1)
            return y.reshape(b, s, h)
        return _moe(x, router_w, w1, w2)
    x = x + _L0_xattn_ref(_layernorm(x, axis=-1), mask_Bx1xSxS_fk0, ctx_2048, L0_xattn_Wq, L0_xattn_Wk, L0_xattn_Wv, L0_xattn_Wo, L0_xattn_gate)
    x = x + _L0_ffn_ref(_layernorm(x, axis=-1), L0_ffn_router_w, L0_ffn_w1, L0_ffn_w2)
    return x

_drawn_inputs = setup_inputs


def setup_inputs(seed=0):
    import zlib

    import numpy as np

    out = dict(_drawn_inputs(seed))
    spreads = {}
    factors = {'ctx_2048': 5.567, 'L0_xattn_Wq': 4.652, 'L0_xattn_Wk': 4.655, 'L0_xattn_gate': 4.49}
    for name, (base, spread) in spreads.items():
        noise = np.random.default_rng([zlib.crc32(name.encode()), seed]).standard_normal(out[name].shape)
        drawn = base * np.exp(spread * noise) if base else spread * noise
        out[name] = jnp.asarray(drawn.astype(out[name].dtype))
    for name, factor in factors.items():
        out[name] = (out[name] * factor).astype(out[name].dtype)
    return out
```

```python
from contextlib import ExitStack

import numpy as np

import concourse.bass as bass
from concourse import mybir

F32, F32R, F16 = mybir.dt.float32, mybir.dt.float32r, mybir.dt.float16
BF16, I32, U32 = mybir.dt.bfloat16, mybir.dt.int32, mybir.dt.uint32
ALU, ACT, AX = mybir.AluOpType, mybir.ActivationFunctionType, mybir.AxisListType

P = 128
NB = 32
T = NB * P
D = 512
NC_ = D // P
NH = 32
HD = D // NH
NE = 8
F = 352
FCH = [(0, 128), (128, 128), (256, 96)]
WS = 64.0
YS = 16.0
EPS = 1e-5
PAIRS = NH // 2
GROUPS = NH // 4
VW = HD + 1
SLOTS = 2 * T // P + NE - 1
TERMS = ((0, 0), (0, 1), (1, 0))


class Batch:

    def __init__(self, it, off, unroll=2):
        self.it, self.off, self.unroll = it, off, unroll
        self.n = unroll * it + off
        self.par = off % 2

    def shift(self, d):
        return Batch(self.it, self.off + d, self.unroll)

    def use(self, buffers):
        return self.unroll // buffers * self.it + self.off // buffers


class Event:

    def __init__(self, sem, per=1):
        self.sem, self.per = sem, per

    def at(self, batch, k=None):
        value = self.per * batch.n + (self.per if k is None else k)
        return max(value, 0) if isinstance(value, int) else value


class Loaded:

    def __init__(self, sems):
        self.sems = sems

    def sem(self, batch):
        return self.sems[batch.off % len(self.sems)]

    def at(self, batch):
        value = 16 * batch.use(len(self.sems)) + 16
        return max(value, 0) if isinstance(value, int) else value


def attention_phase(nc, ctx, dram, keep):
    def sb(name, shape, dt):
        return ctx.enter_context(nc.sbuf_tensor(name, shape, dt))

    def ps(name, shape, dt):
        return ctx.enter_context(nc.psum_tensor(name, shape, dt))

    def ev(name, per=1):
        return Event(ctx.enter_context(nc.semaphore(name)), per)

    def ld(name, n):
        return Loaded([ctx.enter_context(nc.semaphore(f"{name}{k}")) for k in range(n)])

    w1s, count, ident16, held = keep["w1s"], keep["count"], keep["ident16"], keep["held"]

    wts = [sb(f"w_{n}", [P, NC_, 2, D], F16) for n in "qkvo"]
    wq, wk, wv, wo = wts
    identr = sb("identr", [P, P], F32R)
    identf = sb("identf", [P, P], F32)
    ident_bf = sb("ident_bf", [P, P], BF16)
    tri = sb("tri", [P, P], BF16)
    ones = sb("ones", [P, P], BF16)
    hsel = sb("hsel", [3 * NH, NH], BF16)
    rope = sb("rope", [P, 4, HD], F32)
    tg = sb("tg", [P, NH], F32)
    xin = sb("xin", [P, 2, D], F32)
    xres = sb("xres", [P, 2, D], F32)
    cin = sb("cin", [P, D], F32)
    msk = sb("msk", [P, 2, P], F32)
    mskp = sb("mskp", [P, 2, 2, P], F32R)
    stat = sb("stat", [P, 2, 8], F32)
    mv = sb("mv", [P, 2, 4], F32)
    mhalf = sb("mhalf", [P, 1], F32)
    scale = sb("scale", [P, 1], F32)
    xcs = sb("xcs", [P, 2, D], F16)
    xT = sb("xT", [P, 2, NC_, P], F16)
    cT = sb("cT", [P, 2, NC_, P], F16)
    t1 = sb("t1", [P, D], F32)
    t2 = sb("t2", [P, D], F32)
    qs = sb("qs", [P, NH, 4, HD], F16)
    ks = sb("ks", [P, NH, 4, HD], F16)
    aks = sb("aks", [P, NH, 4, HD], F16)
    qz = sb("qz", [P, PAIRS, 2, P], F16)
    kst = sb("kst", [P, PAIRS, P], F16)
    akst = sb("akst", [P, PAIRS, P], F16)
    vv = sb("vv", [P, 2, 2, NH, VW], F32)
    mx = sb("mx", [P, 2, NH], F32)
    mr = sb("mr", [P, 2, NH], F32)
    mp = sb("mp", [P, 2, 3, NH], BF16)
    mT = sb("mT", [3 * NH, 2, P], BF16)
    pr = sb("pr", [P, 2, 4, P], F32)
    avs = sb("avs", [P, NH, 2, VW], F32)
    rc = sb("rc", [P, NH, 2], F32)
    nat = sb("nat", [P, D], F32)
    oT = sb("oT", [P, 2, NC_, P], F16)
    x2 = sb("x2", [P, D], F32)
    ohs = sb("ohs", [P, 2, D], F16)
    hT = sb("hT", [P, 2, NC_, P], F16)
    rwf = sb("rwf", [P, NC_, NE], F32)
    rw = sb("rw", [P, NC_, 2, NE], F16)
    wst = sb("wst", [P, 2 * F], F32)
    lg = sb("lg", [P, NE], F32)
    top = sb("top", [P, 8], F32)
    key = sb("key", [P, 2, NE], F32)
    lowest = sb("lowest", [P, 2], F32)
    gap = sb("gap", [P, 4], F32)
    w2nd = sb("w2nd", [P, 1], F32)
    iota8 = sb("iota8", [P, NE], F32)
    ebase = sb("ebase", [P, NE], F32)
    oh = sb("oh", [P, 2, NE], F32)
    sel = sb("sel", [P, NE], BF16)
    unsel = sb("unsel", [P, NE], F32)
    wsel = sb("wsel", [P, NE], F32)
    tok = sb("tok", [P, 2], F32)
    pos = sb("pos", [P, NE], F32)
    posi = sb("posi", [P, NE], I32)
    row = sb("row", [P, NE, 2], F32)

    st = [ps(f"st{k}", [P, 4, P], F32) for k in range(2)]
    av = [ps(f"av{k}", [P, 8, 2, VW], F32) for k in range(2)]
    ma = [ps(f"ma{k}", [P, 512], F32) for k in range(2)]
    md = [ps(f"md{k}", [P, 512], F32) for k in range(2)]

    def half(bank):
        return bank[:, :].bitcast(F16).rearrange("p (a n) -> p a n", a=8)

    x_in, c_in, m_in, w_in = ld("x_in", 2), ld("c_in", 1), ld("m_in", 2), ld("w_in", 1)
    out_st, h2_st = ld("out_st", 1), ld("h2_st", 1)
    list_st = ev("list_st", 16 * NE)
    const_in, wt_in = [ld(f"const_in{k}", 1) for k in range(3)], [ld(f"wt_in{k}", 1) for k in range(4)]
    pool_c, dve_c, act_c = ev("pool_c"), ev("dve_c"), ev("act_c")
    wt_hi, wt_lo = ev("wt_hi"), ev("wt_lo")
    x_st, x_ag, x_ve, x_rs, x_kept, x_n = (ev(n) for n in ("x_st", "x_ag", "x_ve", "x_rs", "x_kept", "x_n"))
    x_hi, x_lo, x_tp, x_T = ev("x_hi"), ev("x_lo"), ev("x_tp"), ev("x_T")
    c_hi, c_lo, c_tp, c_T = ev("c_hi"), ev("c_lo"), ev("c_tp"), ev("c_T")
    ak_p, av_p, q_p, k_p, v_p = (ev(n) for n in ("ak_p", "av_p", "q_p", "k_p", "v_p"))
    ak_hi, ak_lo, av_v, v_v = ev("ak_hi"), ev("ak_lo"), ev("av_v"), ev("v_v")
    q_t1, q_t2, q_r, q_hi, q_lo = (ev(n) for n in ("q_t1", "q_t2", "q_r", "q_hi", "q_lo"))
    k_t1, k_t2, k_r, k_hi, k_lo = (ev(n) for n in ("k_t1", "k_t2", "k_r", "k_hi", "k_lo"))
    m_hi, m_lo = ev("m_hi"), ev("m_lo")
    w_sc, w_hi, w_lo = ev("w_sc"), ev("w_hi"), ev("w_lo")
    stk_t, stk_v, stk_a = ev("stk_t", 6), ev("stk_v", 3), ev("stk_a", 3)
    s_pe, s_ad, s_own = ev("s_pe", GROUPS), ev("s_ad", GROUPS), ev("s_own", GROUPS)
    mp1, mr1, mp2, mr2, mp3, mp_t, m_T = (ev(n) for n in ("mp1", "mr1", "mp2", "mr2", "mp3", "mp_t", "m_T"))
    t_pe, p_ex, av_pe, av_s = ev("t_pe", 2 * GROUPS), ev("p_ex", 2 * GROUPS), ev("av_pe", 2 * GROUPS), ev("av_s", 4)
    n_rc, n_rg, n_o1, n_o2, n_o = (ev(n) for n in ("n_rc", "n_rg", "n_o1", "n_o2", "n_o"))
    o_hi, o_lo, o_tp, o_T, o_p, x_2 = (ev(n) for n in ("o_hi", "o_lo", "o_tp", "o_T", "o_p", "x_2"))
    h_st, h_ag, h_ve, h_rs, h_n, h_hi, h_lo = (ev(n) for n in ("h_st", "h_ag", "h_ve", "h_rs", "h_n", "h_hi", "h_lo"))
    h_tp, h_T, r_p, r_lg, r_top, r_ex1 = (ev(n) for n in ("h_tp", "h_T", "r_p", "r_lg", "r_top", "r_ex1"))
    r_eq, r_key, r_min, r_oh = (ev(n, 2) for n in ("r_eq", "r_key", "r_min", "r_oh"))
    r_gap, r_ex, r_1, r_w, r_w2 = (ev(n) for n in ("r_gap", "r_ex", "r_1", "r_w", "r_w2"))
    r_sel, r_un, r_wa, r_id, r_row = (ev(n) for n in ("r_sel", "r_un", "r_wa", "r_id", "r_row"))
    f_p, f_c, f_u, f_e, f_pos, f_cnt, f_tok = (ev(n) for n in ("f_p", "f_c", "f_u", "f_e", "f_pos", "f_cnt", "f_tok"))

    block = ctx.enter_context(nc.Block())
    A0 = Batch(0, 0)

    def walk(eng, step, first, last):
        first(Batch(0, 0))
        step(Batch(0, 0), True, False)
        with eng.Fori(0, NB // 2 - 1) as it:
            step(Batch(it, 1), False, False)
            step(Batch(it, 2), False, False)
        step(Batch(0, NB - 1), False, True)
        last(Batch(0, NB - 1))

    def heads(t):
        return t[:, :].rearrange("p (h d) -> p h d", d=HD)

    def twice(t):
        return heads(t).unsqueeze(2).to_broadcast([P, NH, 2, HD])

    def slice_of(n, part):
        return w1s[:, bass.ds(n.n, 1), part, :].rearrange("p a n -> p (a n)")

    def m_bank():
        return st[0][:, :, :].rearrange("p a n -> p (a n)").bitcast(BF16)[:, 0:2 * P].rearrange(
            "p (a n) -> p a n", a=2)

    @block.sync
    def _(sp):
        def load_x(n):
            sp.wait_ge(x_kept.sem, x_kept.at(n.shift(-2)))
            sp.wait_ge(x_n.sem, x_n.at(n.shift(-2)))
            sp.dma_start(xin[:, n.par, :], dram["x"](n)).then_inc(x_in.sem(n), 16)

        def load_c(n):
            sp.wait_ge(c_lo.sem, c_lo.at(n.shift(-1)))
            sp.dma_start(cin[:, :], dram["ctx"](n)).then_inc(c_in.sem(n), 16)

        def load_m(n):
            sp.wait_ge(s_own.sem, s_own.at(n.shift(-2)))
            sp.wait_ge(m_lo.sem, m_lo.at(n.shift(-2)))
            sp.dma_start(msk[:, n.par, :], dram["mask"](n)).then_inc(m_in.sem(n), 16)

        def load_w(n):
            sp.wait_ge(w_lo.sem, w_lo.at(n.shift(-1)))
            sp.dma_start(wst[:, :], dram["w1"](n)).then_inc(w_in.sem(n), 16)

        def store(n):
            sp.wait_ge(x_2.sem, x_2.at(n))
            sp.dma_start(dram["out"](n), x2[:, :]).then_inc(out_st.sem(n), 16)
            sp.wait_ge(h_lo.sem, h_lo.at(n))
            sp.wait_ge(h_hi.sem, h_hi.at(n))
            sp.dma_start(dram["h2"](n), ohs[:, :, :].rearrange("p a n -> p (a n)")).then_inc(h2_st.sem(n), 16)

        for k, n in enumerate((1, 2, 0, 3)):
            stage = keep["stage"](n)
            sp.dma_start(stage, dram["w"][n]).then_inc(wt_in[n].sems[0], 16)
            if k == 0:
                load_c(A0)
                load_x(A0)
                load_m(A0)
                sp.dma_start(rope[:, :, :], dram["rope"]).then_inc(const_in[0].sems[0], 16)
                sp.dma_start(tg[:, :], dram["gate"].to_broadcast([P, NH])).then_inc(const_in[1].sems[0], 16)
                sp.dma_start(rwf[:, :, :], dram["router"]).then_inc(const_in[2].sems[0], 16)
        load_w(A0)

        def step(b, is_first, is_last):
            if not is_last:
                n = b.shift(1)
                load_x(n)
                load_c(n)
                load_m(n)
            if not is_first:
                store(b.shift(-1))
            if not is_last:
                load_w(b.shift(1))

        walk(sp, step, lambda b: None, lambda b: store(b))
        sp.wait_ge(out_st.sem(Batch(0, NB - 1)), out_st.at(Batch(0, NB - 1)))
        sp.wait_ge(h2_st.sem(Batch(0, NB - 1)), h2_st.at(Batch(0, NB - 1)))

    @block.gpsimd
    def _(pool):
        marks = [0]

        def const(ins):
            ins.then_inc(pool_c.sem, 1)
            marks[0] += 1
            pool.wait_ge(pool_c.sem, marks[0])

        const(pool.memset(mhalf[:, :], -0.5))
        const(pool.memset(held[:, 2:4], 1.0))
        const(pool.memset(scale[:, :], WS))
        const(pool.memset(identf[:, :], 1.0))
        const(pool.affine_select(out=identf[:, :], in_=identf[:, :], compare_op=ALU.is_equal, fill=0.0,
                                 base=0, pattern=[[-1, P]], channel_multiplier=1))
        const(pool.memset(vv[:, :, :, :, HD:VW], 1.0))
        const(pool.memset(qz[:, :, :, :], 0.0))
        const(pool.memset(ones[:, :], 1.0))
        const(pool.affine_select(out=tri[:, :], in_=ones[:, :], compare_op=ALU.is_gt, fill=0.0,
                                 base=0, pattern=[[1, P]], channel_multiplier=-1))
        const(pool.memset(hsel[:, :], 0.0))
        for part in range(3):
            const(pool.affine_select(out=hsel[:, :], in_=hsel[:, :], compare_op=ALU.not_equal, fill=1.0,
                                     base=-NH * part, pattern=[[-1, NH]], channel_multiplier=1))
        const(pool.iota(posi[:, 0:NE], pattern=[[1, NE]], base=0, channel_multiplier=0))
        const(pool.tensor_copy(iota8[:, :], posi[:, 0:NE]))
        const(pool.iota(posi[:, 0:1], pattern=[[1, 1]], base=0, channel_multiplier=1))
        const(pool.tensor_copy(tok[:, 0:1], posi[:, 0:1]))
        const(pool.tensor_scalar(tok[:, 1:2], tok[:, 0:1], -1.0, float(T - 1), ALU.mult, ALU.add))
        const(pool.tensor_scalar(ebase[:, :], iota8[:, :], float(T), None, ALU.mult))
        const(pool.memset(count[:, :], 0.0))

        def stage_a(n):
            pool.wait_ge(x_ve.sem, x_ve.at(n))
            pool.tensor_tensor(mv[:, 0, 3:4], mv[:, 0, 2:3], mhalf[:, :], ALU.pow).then_inc(x_rs.sem, 1)

        def keep_x(n):
            pool.wait_ge(x_in.sem(n), x_in.at(n))
            pool.wait_ge(x_2.sem, x_2.at(n.shift(-2)))
            one = held[:, 2:3].to_broadcast([P, D])
            pool.tensor_tensor(xres[:, n.par, :], xin[:, n.par, :], one, ALU.mult).then_inc(x_kept.sem, 1)

        def rotate(n, e1, e2, er, eh, el, high, rest):
            pool.wait_ge(e1.sem, e1.at(n))
            pool.wait_ge(e2.sem, e2.at(n))
            pool.tensor_tensor(t1[:, :], t1[:, :], t2[:, :], ALU.add).then_inc(er.sem, 1)
            pool.wait_ge(eh.sem, eh.at(n))
            pool.wait_ge(er.sem, er.at(n))
            pool.tensor_tensor(rest, twice(t1), high, ALU.subtract).then_inc(el.sem, 1)

        def step(b, is_first, is_last):
            d, n = b.shift(-1), b.shift(1)
            if not is_first:
                own_out(d)
            if not is_last:
                stage_a(n)
            if not is_first:
                norm_h(d)
            if not is_last:
                keep_x(n)
            w_slice(b)
            if not is_last:
                rotate(n, q_t1, q_t2, q_r, q_hi, q_lo, qs[:, :, 0:2, :], qs[:, :, 2:4, :])
                rotate(n, k_t1, k_t2, k_r, k_hi, k_lo, ks[:, :, 0:4:2, :], ks[:, :, 1:4:2, :])
            if not is_first:
                enter_lists(d)

        def w_slice(n):
            pool.wait_ge(w_in.sem(n), w_in.at(n))
            by = scale[:, :].to_broadcast([P, 2 * F])
            pool.tensor_tensor(wst[:, :], wst[:, :], by, ALU.mult).then_inc(w_sc.sem, 1)
            pool.wait_ge(w_hi.sem, w_hi.at(n))
            pool.wait_ge(w_sc.sem, w_sc.at(n))
            pool.tensor_tensor(slice_of(n, 1), wst[:, :], slice_of(n, 0),
                               ALU.subtract).then_inc(w_lo.sem, 1)

        def own_out(n):
            pool.wait_ge(n_rc.sem, n_rc.at(n))
            pool.tensor_tensor(avs[:, :, 0, 0:HD], avs[:, :, 0, 0:HD],
                               rc[:, :, 0:1].to_broadcast([P, NH, HD]), ALU.mult).then_inc(n_o1.sem, 1)

        def norm_h(n):
            pool.wait_ge(h_ve.sem, h_ve.at(n))
            pool.tensor_tensor(mv[:, 1, 3:4], mv[:, 1, 2:3], mhalf[:, :], ALU.pow).then_inc(h_rs.sem, 1)

        def enter_lists(n):
            pool.wait_ge(f_pos.sem, f_pos.at(n))
            pool.wait_ge(r_row.sem, r_row.at(n))
            pool.wait_ge(r_id.sem, r_id.at(n))
            pool.tensor_tensor(held[:, 1:2], held[:, 2:3], held[:, 2:3], ALU.add)
            for e in range(NE):
                pool.indirect_dma_start(
                    out=dram["lists"], out_offset=bass.IndirectOffsetOnAxis(ap=posi[:, e:e + 1], axis=0),
                    in_=row[:, e, :], in_offset=None).then_inc(list_st.sem, 16)

        def first(n):
            stage_a(n)
            keep_x(n)
            rotate(n, q_t1, q_t2, q_r, q_hi, q_lo, qs[:, :, 0:2, :], qs[:, :, 2:4, :])
            rotate(n, k_t1, k_t2, k_r, k_hi, k_lo, ks[:, :, 0:4:2, :], ks[:, :, 1:4:2, :])

        def last(n):
            own_out(n)
            norm_h(n)
            enter_lists(n)

        walk(pool, step, first, last)
        pool.wait_ge(list_st.sem, list_st.at(Batch(0, NB - 1)))

    @block.scalar
    def _(act):
        def ctx_hi(n):
            act.wait_ge(c_in.sem(n), c_in.at(n))
            act.wait_ge(x_tp.sem, x_tp.at(n.shift(-1)))
            act.activation(xcs[:, 0, :], cin[:, :], ACT.Copy).then_inc(c_hi.sem, 1)

        act.wait_ge(const_in[1].sem(A0), const_in[1].at(A0))
        act.activation(tg[:, :], tg[:, :], ACT.Tanh).then_inc(act_c.sem, 1)
        for k, n in enumerate((1, 2, 0, 3)):
            act.wait_ge(wt_in[n].sem(A0), wt_in[n].at(A0))
            act.activation(wts[n][:, :, 0, :], keep["stage"](n), ACT.Copy, scale=WS).then_inc(wt_hi.sem, 1)
            if k == 0:
                ctx_hi(A0)
        act.wait_ge(const_in[2].sem(A0), const_in[2].at(A0))
        act.activation(rw[:, :, 0, :], rwf[:, :, :], ACT.Copy, scale=WS).then_inc(act_c.sem, 1)

        def stage_a1(n):
            ctx_T(n)
            act.wait_ge(ak_p.sem, ak_p.at(n))
            act.wait_ge(stk_t.sem, stk_t.at(n.shift(-1)))
            act.activation(aks[:, :, 0:4:2, :], twice(ma[1]), ACT.Copy, scale=1 / WS).then_inc(ak_hi.sem, 1)
            act.wait_ge(x_n.sem, x_n.at(n))
            act.wait_ge(c_tp.sem, c_tp.at(n))
            act.activation(xcs[:, 0, :], nat[:, :], ACT.Copy).then_inc(x_hi.sem, 1)
            act.wait_ge(av_p.sem, av_p.at(n))
            act.wait_ge(av_pe.sem, av_pe.at(n.shift(-2)))
            act.activation(vv[:, n.par, 1, :, 0:HD], heads(ma[0]), ACT.Copy, scale=1 / WS).then_inc(av_v.sem, 1)
            act.wait_ge(x_tp.sem, x_tp.at(n))
            act.wait_ge(v_p.sem, v_p.at(n.shift(-1)))
            act.activation(xT[:, :, :, :].rearrange("p a c n -> p (a c) n"), half(ma[1]),
                           ACT.Copy).then_inc(x_T.sem, 1)

        def ctx_T(n):
            act.wait_ge(c_tp.sem, c_tp.at(n))
            act.wait_ge(av_p.sem, av_p.at(n.shift(-1)))
            act.activation(cT[:, :, :, :].rearrange("p a c n -> p (a c) n"), half(ma[0]),
                           ACT.Copy).then_inc(c_T.sem, 1)

        def mask_hi(n):
            act.wait_ge(m_in.sem(n), m_in.at(n))
            act.wait_ge(t_pe.sem, t_pe.at(n.shift(-2)))
            act.activation(mskp[:, n.par, 0, :], msk[:, n.par, :], ACT.Copy).then_inc(m_hi.sem, 1)

        def stage_a2(n):
            act.wait_ge(q_r.sem, q_r.at(n))
            act.wait_ge(stk_t.sem, stk_t.at(n.shift(-1), 2))
            act.activation(qs[:, :, 0:2, :], twice(t1), ACT.Copy).then_inc(q_hi.sem, 1)

        def stage_a3(n):
            act.wait_ge(k_r.sem, k_r.at(n))
            act.wait_ge(stk_t.sem, stk_t.at(n.shift(-1), 4))
            act.activation(ks[:, :, 0:4:2, :], twice(t1), ACT.Copy).then_inc(k_hi.sem, 1)
            act.wait_ge(v_p.sem, v_p.at(n))
            act.activation(vv[:, n.par, 0, :, 0:HD], heads(ma[0]), ACT.Copy, scale=1 / WS).then_inc(v_v.sem, 1)

        def stacks(n):
            s_pe_done = n.shift(-1)
            act.wait_ge(t_pe.sem, t_pe.at(s_pe_done))
            act.wait_ge(stk_t.sem, stk_t.at(n, 2))
            for j in range(2):
                r = slice(64 * j, 64 * j + 64)
                i = act.activation(qz[r, 8:16, j, :], half(ma[1])[r], ACT.Copy)
            i.then_inc(stk_a.sem, 1)
            act.wait_ge(stk_t.sem, stk_t.at(n, 4))
            act.activation(kst[:, 8:16, :], half(ma[1]), ACT.Copy).then_inc(stk_a.sem, 1)
            act.wait_ge(stk_t.sem, stk_t.at(n, 6))
            act.activation(akst[:, 8:16, :], half(ma[1]), ACT.Copy).then_inc(stk_a.sem, 1)

        def exps(n, g, path):
            u = 2 * g + path
            act.wait_ge(t_pe.sem, t_pe.at(n, u + 1))
            act.wait_ge(av_pe.sem, av_pe.at(n, u - 1))
            act.activation(pr[:, path, :, :], st[path][:, :, :], ACT.Exp).then_inc(p_ex.sem, 1)

        def w_slice(n):
            act.wait_ge(w_sc.sem, w_sc.at(n))
            act.activation(slice_of(n, 0), wst[:, :], ACT.Copy).then_inc(w_hi.sem, 1)

        def out_hi(n):
            act.wait_ge(n_o.sem, n_o.at(n))
            act.wait_ge(h_tp.sem, h_tp.at(n.shift(-1)))
            act.wait_ge(h2_st.sem(n.shift(-1)), h2_st.at(n.shift(-1)))
            act.activation(ohs[:, 0, :], nat[:, :], ACT.Copy).then_inc(o_hi.sem, 1)

        def out_T(n):
            act.wait_ge(o_tp.sem, o_tp.at(n))
            act.wait_ge(o_p.sem, o_p.at(n.shift(-1)))
            act.activation(oT[:, :, :, :].rearrange("p a c n -> p (a c) n"), half(md[0]),
                           ACT.Copy).then_inc(o_T.sem, 1)

        def h_high(n):
            act.wait_ge(h_n.sem, h_n.at(n))
            act.wait_ge(o_tp.sem, o_tp.at(n))
            act.activation(ohs[:, 0, :], nat[:, :], ACT.Copy).then_inc(h_hi.sem, 1)

        def router_exp(n):
            act.wait_ge(r_gap.sem, r_gap.at(n))
            act.activation(gap[:, 1:2], gap[:, 0:1], ACT.Exp, scale=1 / WS).then_inc(r_ex.sem, 1)

        def step(b, is_first, is_last):
            d, n = b.shift(-1), b.shift(1)
            if not is_first:
                out_hi(d)
            stacks(b)
            if not is_first:
                out_T(d)
            if not is_last:
                ctx_hi(n)
                mask_hi(n)
                stage_a1(n)
            if not is_first:
                h_high(d)
            w_slice(b)
            if not is_last:
                stage_a2(n)
            for g in range(GROUPS):
                if g == 1 and not is_first:
                    router_exp(d)
                if g == 4 and not is_last:
                    stage_a3(n)
                exps(b, g, 0)
                exps(b, g, 1)

        def first(n):
            mask_hi(n)
            stage_a1(n)
            stage_a2(n)
            stage_a3(n)

        def last(n):
            out_hi(n)
            out_T(n)
            h_high(n)
            router_exp(n)

        walk(act, step, first, last)

    @block.vector
    def _(dve):
        def ctx_lo(n):
            dve.wait_ge(c_hi.sem, c_hi.at(n))
            dve.tensor_tensor(xcs[:, 1, :], cin[:, :], xcs[:, 0, :], ALU.subtract).then_inc(c_lo.sem, 1)

        def mask_lo(n):
            dve.wait_ge(m_hi.sem, m_hi.at(n))
            dve.tensor_tensor(mskp[:, n.par, 1, :], msk[:, n.par, :], mskp[:, n.par, 0, :].bitcast(F32),
                              ALU.subtract).then_inc(m_lo.sem, 1)

        def norm_x(n):
            dve.wait_ge(x_in.sem(n), x_in.at(n))
            dve.bn_stats(stat[:, 0, 0:6], xin[:, n.par, :]).then_inc(x_st.sem, 1)
            dve.wait_ge(x_st.sem, x_st.at(n))
            dve.memset(held[:, 0:1], 0.0)
            dve.bn_aggr(mv[:, 0, 0:2], stat[:, 0, 0:6]).then_inc(x_ag.sem, 1)
            dve.wait_ge(x_ag.sem, x_ag.at(n))
            dve.tensor_scalar(mv[:, 0, 2:3], mv[:, 0, 1:2], EPS, None, ALU.add).then_inc(x_ve.sem, 1)
            dve.wait_ge(x_rs.sem, x_rs.at(n))
            dve.wait_ge(o_hi.sem, o_hi.at(n.shift(-2)))
            dve.wait_ge(o_lo.sem, o_lo.at(n.shift(-2)))
            dve.tensor_scalar(nat[:, :], xin[:, n.par, :], mv[:, 0, 0:1], mv[:, 0, 3:4], ALU.subtract,
                              ALU.mult).then_inc(x_n.sem, 1)

        pool_c_all = 20
        dve.wait_ge(pool_c.sem, pool_c_all)
        dve.tensor_copy(ident16[:, :], identf[:, :]).then_inc(dve_c.sem, 1)
        dve.tensor_copy(identr[:, :], identf[:, :]).then_inc(dve_c.sem, 1)
        dve.tensor_copy(ident_bf[:, :], identf[:, :]).then_inc(dve_c.sem, 1)
        for k, n in enumerate((1, 2, 0, 3)):
            if k == 1:
                ctx_lo(A0)
                mask_lo(A0)
                norm_x(A0)
            dve.wait_ge(wt_hi.sem, k + 1)
            dve.scalar_tensor_tensor(out=wts[n][:, :, 1, :], in0=keep["stage"](n), scalar=WS,
                                     in1=wts[n][:, :, 0, :], op0=ALU.mult, op1=ALU.subtract).then_inc(wt_lo.sem, 1)
        dve.wait_ge(act_c.sem, 2)
        dve.scalar_tensor_tensor(out=rw[:, :, 1, :], in0=rwf[:, :, :], scalar=WS, in1=rw[:, :, 0, :],
                                 op0=ALU.mult, op1=ALU.subtract).then_inc(dve_c.sem, 1)
        dve.wait_ge(const_in[0].sem(A0), const_in[0].at(A0))

        def ak_low(n):
            dve.wait_ge(ak_hi.sem, ak_hi.at(n))
            for j in range(2):
                i = dve.scalar_tensor_tensor(out=aks[:, :, 2 * j + 1, :], in0=heads(ma[1]), scalar=1 / WS,
                                             in1=aks[:, :, 0, :], op0=ALU.mult, op1=ALU.subtract)
            i.then_inc(ak_lo.sem, 1)

        def x_low(n):
            dve.wait_ge(x_hi.sem, x_hi.at(n))
            dve.tensor_tensor(xcs[:, 1, :], nat[:, :], xcs[:, 0, :], ALU.subtract).then_inc(x_lo.sem, 1)

        def rotate(n, tab, bank, proj, e1, e2, free):
            dve.wait_ge(proj.sem, proj.at(n))
            free()
            cos = rope[:, tab, :].unsqueeze(1).to_broadcast([P, NH, HD])
            dve.tensor_tensor(heads(t1), heads(bank), cos, ALU.mult).then_inc(e1.sem, 1)
            for j in range(2):
                a, z = slice(8 * j, 8 * j + 8), slice(8 - 8 * j, 16 - 8 * j)
                sin = rope[:, tab + 1, a].unsqueeze(1).to_broadcast([P, NH, HD // 2])
                i = dve.tensor_tensor(heads(t2)[:, :, a], heads(bank)[:, :, z], sin, ALU.mult)
            i.then_inc(e2.sem, 1)

        def rotate_q(n):
            def free():
                dve.wait_ge(k_lo.sem, k_lo.at(n.shift(-1)))
                dve.wait_ge(k_hi.sem, k_hi.at(n.shift(-1)))
            rotate(n, 0, ma[0], q_p, q_t1, q_t2, free)

        def rotate_k(n):
            def free():
                dve.wait_ge(q_lo.sem, q_lo.at(n))
                dve.wait_ge(q_hi.sem, q_hi.at(n))
            rotate(n, 2, ma[1], k_p, k_t1, k_t2, free)

        def stacks(n):
            dve.wait_ge(t_pe.sem, t_pe.at(n.shift(-1)))
            dve.wait_ge(stk_t.sem, stk_t.at(n, 1))
            for j in range(2):
                r = slice(64 * j, 64 * j + 64)
                i = dve.tensor_copy(qz[r, 0:8, j, :], half(ma[0])[r])
            i.then_inc(stk_v.sem, 1)
            dve.wait_ge(stk_t.sem, stk_t.at(n, 3))
            dve.tensor_copy(kst[:, 0:8, :], half(ma[0])).then_inc(stk_v.sem, 1)
            dve.wait_ge(stk_t.sem, stk_t.at(n, 5))
            dve.tensor_copy(akst[:, 0:8, :], half(ma[0])).then_inc(stk_v.sem, 1)

        def maxima(n, g):
            dve.wait_ge(s_pe.sem, s_pe.at(n, g + 1))
            dve.wait_ge(s_own.sem, s_own.at(n, g))
            dve.tensor_reduce(mx[:, 1, 4 * g:4 * g + 4], st[1][:, :, :], AX.X, ALU.max).then_inc(s_ad.sem, 1)
            for j in range(4):
                h = 4 * g + j
                i = dve.tensor_tensor_reduce(st[0][:, j, :], st[0][:, j, :], msk[:, n.par, :], 1.0, -3.4028235e38,
                                             ALU.add, ALU.max, mx[:, 0, h:h + 1])
            i.then_inc(s_own.sem, 1)

        def neg_max(n):
            dve.wait_ge(s_own.sem, s_own.at(n))
            dve.wait_ge(s_ad.sem, s_ad.at(n))
            dve.wait_ge(mp_t.sem, mp_t.at(n.shift(-1)))
            p3 = [mp[:, :, k, :] for k in range(3)]
            dve.tensor_scalar(p3[0], mx[:, :, :], -1.0, None, ALU.mult).then_inc(mp1.sem, 1)
            dve.wait_ge(mp1.sem, mp1.at(n))
            dve.scalar_tensor_tensor(out=mr[:, :, :], in0=mx[:, :, :], scalar=-1.0, in1=p3[0],
                                     op0=ALU.mult, op1=ALU.subtract).then_inc(mr1.sem, 1)
            dve.wait_ge(mr1.sem, mr1.at(n))
            dve.tensor_copy(p3[1], mr[:, :, :]).then_inc(mp2.sem, 1)
            dve.wait_ge(mp2.sem, mp2.at(n))
            dve.tensor_tensor(mr[:, :, :], mr[:, :, :], p3[1], ALU.subtract).then_inc(mr2.sem, 1)
            dve.wait_ge(mr2.sem, mr2.at(n))
            dve.tensor_copy(p3[2], mr[:, :, :]).then_inc(mp3.sem, 1)
            dve.wait_ge(mp_t.sem, mp_t.at(n))
            dve.tensor_copy(mT[:, :, :], m_bank()[0:3 * NH]).then_inc(m_T.sem, 1)

        def values_out(n, o):
            dve.wait_ge(av_pe.sem, av_pe.at(n, 4 * o + 4))
            if o == 0:
                dve.wait_ge(n_o.sem, n_o.at(n.shift(-1)))
            dve.tensor_copy(avs[:, 8 * o:8 * o + 8, :, :], av[o % 2][:, :, :, :]).then_inc(av_s.sem, 1)

        def norm_out(n):
            dve.wait_ge(av_s.sem, av_s.at(n))
            dve.reciprocal(rc[:, :, :], avs[:, :, :, HD]).then_inc(n_rc.sem, 1)
            dve.wait_ge(n_rc.sem, n_rc.at(n))
            dve.tensor_tensor(rc[:, :, 1], rc[:, :, 1], tg[:, :], ALU.mult).then_inc(n_rg.sem, 1)
            dve.wait_ge(n_rg.sem, n_rg.at(n))
            dve.tensor_tensor(avs[:, :, 1, 0:HD], avs[:, :, 1, 0:HD],
                              rc[:, :, 1:2].to_broadcast([P, NH, HD]), ALU.mult).then_inc(n_o2.sem, 1)
            dve.wait_ge(n_o1.sem, n_o1.at(n))
            dve.wait_ge(n_o2.sem, n_o2.at(n))
            dve.wait_ge(h_hi.sem, h_hi.at(n.shift(-1)))
            dve.wait_ge(h_lo.sem, h_lo.at(n.shift(-1)))
            dve.tensor_tensor(heads(nat), avs[:, :, 0, 0:HD], avs[:, :, 1, 0:HD], ALU.add).then_inc(n_o.sem, 1)

        def out_low(n):
            dve.wait_ge(o_hi.sem, o_hi.at(n))
            dve.tensor_tensor(ohs[:, 1, :], nat[:, :], ohs[:, 0, :], ALU.subtract).then_inc(o_lo.sem, 1)

        def residual(n):
            dve.wait_ge(o_p.sem, o_p.at(n))
            dve.wait_ge(x_kept.sem, x_kept.at(n))
            dve.wait_ge(out_st.sem(n.shift(-1)), out_st.at(n.shift(-1)))
            dve.scalar_tensor_tensor(out=x2[:, :], in0=md[1][:, :], scalar=1 / WS, in1=xres[:, n.par, :],
                                     op0=ALU.mult, op1=ALU.add).then_inc(x_2.sem, 1)
            dve.wait_ge(x_2.sem, x_2.at(n))
            dve.bn_stats(stat[:, 1, 0:6], x2[:, :]).then_inc(h_st.sem, 1)
            dve.wait_ge(h_st.sem, h_st.at(n))
            dve.memset(held[:, 0:1], 0.0)
            dve.bn_aggr(mv[:, 1, 0:2], stat[:, 1, 0:6]).then_inc(h_ag.sem, 1)
            dve.wait_ge(h_ag.sem, h_ag.at(n))
            dve.tensor_scalar(mv[:, 1, 2:3], mv[:, 1, 1:2], EPS, None, ALU.add).then_inc(h_ve.sem, 1)

        def norm_h(n, x_batch):
            dve.wait_ge(h_rs.sem, h_rs.at(n))
            if x_batch:
                dve.wait_ge(x_hi.sem, x_hi.at(x_batch))
                dve.wait_ge(x_lo.sem, x_lo.at(x_batch))
            dve.wait_ge(o_hi.sem, o_hi.at(n))
            dve.wait_ge(o_lo.sem, o_lo.at(n))
            dve.tensor_scalar(nat[:, :], x2[:, :], mv[:, 1, 0:1], mv[:, 1, 3:4], ALU.subtract,
                              ALU.mult).then_inc(h_n.sem, 1)

        def h_low(n):
            dve.wait_ge(h_hi.sem, h_hi.at(n))
            dve.tensor_tensor(ohs[:, 1, :], nat[:, :], ohs[:, 0, :], ALU.subtract).then_inc(h_lo.sem, 1)

        def h_transposed(n):
            dve.wait_ge(h_tp.sem, h_tp.at(n))
            dve.wait_ge(r_p.sem, r_p.at(n.shift(-1)))
            dve.tensor_copy(hT[:, :, :, :].rearrange("p a c n -> p (a c) n"), half(md[0])).then_inc(h_T.sem, 1)

        def router_top(n):
            dve.wait_ge(r_p.sem, r_p.at(n))
            dve.tensor_copy(lg[:, :], md[1][:, 0:NE]).then_inc(r_lg.sem, 1)
            dve.wait_ge(r_lg.sem, r_lg.at(n))
            dve.memset(held[:, 0:1], 0.0)
            dve.max(top[:, :], lg[:, :]).then_inc(r_top.sem, 1)
            dve.wait_ge(r_top.sem, r_top.at(n))
            dve.tensor_tensor(gap[:, 0:1], top[:, 1:2], top[:, 0:1], ALU.subtract).then_inc(r_gap.sem, 1)
            for k in range(2):
                dve.tensor_scalar(key[:, k, :], lg[:, :], top[:, k:k + 1], -float(NE), ALU.is_equal,
                                  ALU.mult).then_inc(r_eq.sem, 1)
                dve.wait_ge(r_eq.sem, r_eq.at(n, k + 1))
                dve.tensor_tensor(key[:, k, :], key[:, k, :], iota8[:, :], ALU.add).then_inc(r_key.sem, 1)
                dve.wait_ge(r_key.sem, r_key.at(n, k + 1))
                if k:
                    dve.scalar_tensor_tensor(out=key[:, k, :], in0=oh[:, 0, :], scalar=2.0 * NE,
                                             in1=key[:, k, :], op0=ALU.mult, op1=ALU.add).then_inc(r_ex1.sem, 1)
                    dve.wait_ge(r_ex1.sem, r_ex1.at(n))
                dve.tensor_reduce(lowest[:, k:k + 1], key[:, k, :], AX.X, ALU.min).then_inc(r_min.sem, 1)
                dve.wait_ge(r_min.sem, r_min.at(n, k + 1))
                dve.tensor_scalar(oh[:, k, :], iota8[:, :], -float(NE), lowest[:, k:k + 1], ALU.add,
                                  ALU.is_equal).then_inc(r_oh.sem, 1)
                dve.wait_ge(r_oh.sem, r_oh.at(n, k + 1))
            dve.wait_ge(f_p.sem, f_p.at(n.shift(-1)))
            dve.tensor_tensor(sel[:, :], oh[:, 0, :], oh[:, 1, :], ALU.add).then_inc(r_sel.sem, 1)

        def router_weights(n):
            dve.wait_ge(r_ex.sem, r_ex.at(n))
            dve.tensor_scalar(gap[:, 2:3], gap[:, 1:2], 1.0, None, ALU.add).then_inc(r_1.sem, 1)
            dve.wait_ge(r_1.sem, r_1.at(n))
            dve.reciprocal(gap[:, 3:4], gap[:, 2:3]).then_inc(r_w.sem, 1)
            dve.wait_ge(r_w.sem, r_w.at(n))
            dve.tensor_tensor(w2nd[:, :], gap[:, 1:2], gap[:, 3:4], ALU.mult).then_inc(r_w2.sem, 1)
            dve.tensor_scalar(wsel[:, :], oh[:, 0, :], gap[:, 3:4], None, ALU.mult).then_inc(r_wa.sem, 1)
            dve.wait_ge(r_w2.sem, r_w2.at(n))
            dve.wait_ge(r_wa.sem, r_wa.at(n))
            dve.wait_ge(list_st.sem, list_st.at(n.shift(-1)))
            dve.scalar_tensor_tensor(out=row[:, :, 1], in0=oh[:, 1, :], scalar=w2nd[:, :], in1=wsel[:, :],
                                     op0=ALU.mult, op1=ALU.add).then_inc(r_row.sem, 1)
            dve.tensor_copy(row[:, :, :].bitcast(I32)[:, :, 0], tok[:, 0:1].to_broadcast([P, NE])).then_inc(r_id.sem, 1)
            dve.tensor_scalar(unsel[:, :], sel[:, :], -1.0, 1.0, ALU.mult, ALU.add).then_inc(r_un.sem, 1)
            dve.wait_ge(f_p.sem, f_p.at(n))
            dve.tensor_tensor(pos[:, :], md[0][:, 0:NE], count[:, :], ALU.add).then_inc(f_c.sem, 1)
            dve.wait_ge(f_c.sem, f_c.at(n))
            dve.wait_ge(r_un.sem, r_un.at(n))
            dve.tensor_tensor(count[:, :], md[0][:, NE:2 * NE], count[:, :], ALU.add).then_inc(f_cnt.sem, 1)
            dve.scalar_tensor_tensor(out=pos[:, :], in0=unsel[:, :], scalar=tok[:, 1:2], in1=pos[:, :],
                                     op0=ALU.mult, op1=ALU.add).then_inc(f_u.sem, 1)
            dve.wait_ge(f_u.sem, f_u.at(n))
            dve.tensor_tensor(pos[:, :], pos[:, :], ebase[:, :], ALU.add).then_inc(f_e.sem, 1)
            dve.wait_ge(f_e.sem, f_e.at(n))
            dve.tensor_copy(posi[:, :], pos[:, :]).then_inc(f_pos.sem, 1)
            dve.tensor_scalar(tok[:, 0:1], tok[:, 0:1], float(P), None, ALU.add)
            dve.tensor_scalar(tok[:, 1:2], tok[:, 1:2], float(-P), None, ALU.add).then_inc(f_tok.sem, 1)
            dve.wait_ge(f_tok.sem, f_tok.at(n))

        def step(b, is_first, is_last):
            d, n = b.shift(-1), b.shift(1)
            if not is_first:
                out_low(d)
            stacks(b)
            if not is_last:
                ctx_lo(n)
                mask_lo(n)
            for g in range(GROUPS):
                if g == 1 and not is_last:
                    norm_x(n)
                if g == 3 and not is_first:
                    residual(d)
                if g == 3 and not is_last:
                    ak_low(n)
                if g == 4 and not is_last:
                    x_low(n)
                if g == 4 and not is_first:
                    norm_h(d, None if is_last else n)
                if g == 6 and not is_first:
                    h_low(d)
                maxima(b, g)
            if not is_last:
                rotate_q(n)
            neg_max(b)
            if not is_first:
                h_transposed(d)
                router_top(d)
            values_out(b, 0)
            if not is_last:
                rotate_k(n)
            if not is_first:
                router_weights(d)
            for o in range(1, 4):
                values_out(b, o)
            norm_out(b)

        def first(n):
            ak_low(n)
            x_low(n)
            rotate_q(n)
            rotate_k(n)

        def last(n):
            out_low(n)
            residual(n)
            norm_h(n, None)
            h_low(n)
            h_transposed(n)
            router_top(n)
            router_weights(n)

        walk(dve, step, first, last)

    @block.tensor
    def _(pe):
        def transposes(bank, src):
            for part in range(2):
                for c in range(NC_):
                    i = pe.transpose(half(bank)[:, part * NC_ + c, :], src[:, part, c * P:(c + 1) * P], ident16[:, :])
            return i

        def project(bank, xt, w, cols=D):
            n = 0
            for a, z in TERMS:
                for c in range(NC_):
                    i = pe.matmul(bank[:, 0:cols], xt[:, a, c, :], w[:, c, z, :], start=(n == 0), stop=(n == 11))
                    n += 1
            return i

        def wait_weight(k):
            pe.wait_ge(wt_lo.sem, k)

        def ctx_turn(n):
            pe.wait_ge(c_hi.sem, c_hi.at(n))
            pe.wait_ge(c_lo.sem, c_lo.at(n))
            pe.wait_ge(stk_v.sem, stk_v.at(n.shift(-1)))
            transposes(ma[0], xcs).then_inc(c_tp.sem, 1)

        def ak(n):
            pe.wait_ge(c_T.sem, c_T.at(n))
            pe.wait_ge(stk_a.sem, stk_a.at(n.shift(-1)))
            project(ma[1], cT, wk).then_inc(ak_p.sem, 1)

        def avp(n):
            project(ma[0], cT, wv).then_inc(av_p.sem, 1)

        def x_turn(n):
            pe.wait_ge(x_hi.sem, x_hi.at(n))
            pe.wait_ge(x_lo.sem, x_lo.at(n))
            pe.wait_ge(ak_lo.sem, ak_lo.at(n))
            transposes(ma[1], xcs).then_inc(x_tp.sem, 1)

        def q(n):
            pe.wait_ge(x_T.sem, x_T.at(n))
            pe.wait_ge(av_v.sem, av_v.at(n))
            project(ma[0], xT, wq).then_inc(q_p.sem, 1)

        def k(n):
            project(ma[1], xT, wk).then_inc(k_p.sem, 1)

        def v(n):
            pe.wait_ge(q_t1.sem, q_t1.at(n))
            pe.wait_ge(q_t2.sem, q_t2.at(n))
            project(ma[0], xT, wv).then_inc(v_p.sem, 1)

        def stack(src, bank, p0):
            for p in range(8):
                pair = src[:, 2 * (p0 + p):2 * (p0 + p) + 2, :, :].rearrange("q h a d -> q (h a d)")
                i = pe.transpose(half(bank)[:, p, :], pair, ident16[:, :])
            i.then_inc(stk_t.sem, 1)

        def stacks(n):
            pe.wait_ge(v_v.sem, v_v.at(n))
            pe.wait_ge(q_lo.sem, q_lo.at(n))
            pe.wait_ge(k_t2.sem, k_t2.at(n))
            pe.wait_ge(k_t1.sem, k_t1.at(n))
            stack(qs, ma[0], 0)
            stack(qs, ma[1], 8)
            pe.wait_ge(k_lo.sem, k_lo.at(n))
            pe.wait_ge(stk_v.sem, stk_v.at(n, 1))
            stack(ks, ma[0], 0)
            pe.wait_ge(stk_a.sem, stk_a.at(n, 1))
            stack(ks, ma[1], 8)
            pe.wait_ge(stk_v.sem, stk_v.at(n, 2))
            pe.wait_ge(ak_lo.sem, ak_lo.at(n))
            stack(aks, ma[0], 0)
            pe.wait_ge(stk_a.sem, stk_a.at(n, 2))
            stack(aks, ma[1], 8)

        def scores(n, g):
            if g == 0:
                pe.wait_ge(stk_v.sem, stk_v.at(n, 3))
                pe.wait_ge(stk_a.sem, stk_a.at(n, 3))
                pe.wait_ge(p_ex.sem, p_ex.at(n.shift(-1)))
            pe.wait_ge(s_own.sem, s_own.at(n, g))
            pe.wait_ge(s_ad.sem, s_ad.at(n, g))
            for path, keys in ((0, kst), (1, akst)):
                for j in range(4):
                    h = 4 * g + j
                    i = pe.matmul(st[path][:, j, :], qz[:, h // 2, h % 2, :], keys[:, h // 2, :],
                                  start=True, stop=True)
            i.then_inc(s_pe.sem, 1)

        def max_turn(n):
            pe.wait_ge(mp3.sem, mp3.at(n))
            for path in range(2):
                i = pe.transpose(m_bank()[0:3 * NH, path, :], mp[:, path, :, :].rearrange("p a h -> p (a h)"),
                                 ident_bf[:, :])
            i.then_inc(mp_t.sem, 1)

        def scores_T(n, g, path):
            u = 2 * g + path
            if u == 0:
                pe.wait_ge(m_T.sem, m_T.at(n))
                pe.wait_ge(m_lo.sem, m_lo.at(n))
                pe.wait_ge(m_hi.sem, m_hi.at(n))
            if u >= 2:
                pe.wait_ge(p_ex.sem, p_ex.at(n, u - 1))
            bank, keys = st[path], (kst, akst)[path]
            for j in range(2):
                p = 2 * g + j
                pe.matmul(bank[:, 2 * j:2 * j + 2, :], keys[:, p, :], qz[:, p, :, :], start=(j == 0), stop=False,
                          skip_group_check=True)
            if path == 0:
                for part in range(2):
                    pe.matmul(bank[:, :, :], mskp[:, n.par, part, :],
                              identr[:, :].unsqueeze(1).to_broadcast([P, 4, P]), start=False, stop=False,
                              skip_group_check=True)
            for j in range(4):
                h = 4 * g + j
                i = pe.matmul(bank[:, j, :], hsel[:, h:h + 1].to_broadcast([3 * NH, P]), mT[:, path, :],
                              start=False, stop=(j == 3), skip_group_check=True)
            i.then_inc(t_pe.sem, 1)

        def values(n, g, path):
            u = 2 * g + path
            pe.wait_ge(p_ex.sem, p_ex.at(n, u + 1))
            if u == 0:
                pe.wait_ge(av_v.sem, av_v.at(n))
                pe.wait_ge(v_v.sem, v_v.at(n))
            o = g // 2
            if u % 4 == 0:
                pe.wait_ge(av_s.sem, av_s.at(n, o - 1))
            for j in range(4):
                h = 4 * g + j
                i = pe.matmul(av[o % 2][:, h % 8, path, :], pr[:, path, j, :], vv[:, n.par, path, h, :],
                              start=True, stop=True)
            i.then_inc(av_pe.sem, 1)

        def out_turn(n):
            pe.wait_ge(o_hi.sem, o_hi.at(n))
            pe.wait_ge(o_lo.sem, o_lo.at(n))
            pe.wait_ge(f_cnt.sem, f_cnt.at(n.shift(-1)))
            pe.wait_ge(f_c.sem, f_c.at(n.shift(-1)))
            transposes(md[0], ohs).then_inc(o_tp.sem, 1)

        def out_project(n):
            pe.wait_ge(o_T.sem, o_T.at(n))
            pe.wait_ge(r_lg.sem, r_lg.at(n.shift(-1)))
            project(md[1], oT, wo).then_inc(o_p.sem, 1)

        def h_turn(n):
            pe.wait_ge(h_lo.sem, h_lo.at(n))
            pe.wait_ge(h_hi.sem, h_hi.at(n))
            transposes(md[0], ohs).then_inc(h_tp.sem, 1)

        def router(n):
            pe.wait_ge(h_T.sem, h_T.at(n))
            project(md[1], hT, rw, NE).then_inc(r_p.sem, 1)

        def places(n):
            pe.wait_ge(r_sel.sem, r_sel.at(n))
            pe.matmul(md[0][:, 0:NE], tri[:, :], sel[:, :], start=True, stop=True)
            pe.matmul(md[0][:, NE:2 * NE], ones[:, :], sel[:, :], start=True, stop=True).then_inc(f_p.sem, 1)

        def step(b, is_first, is_last):
            d, n = b.shift(-1), b.shift(1)
            stacks(b)
            if not is_first:
                out_turn(d)
            for g in range(GROUPS):
                scores(b, g)
                if g == 0 and not is_last:
                    ctx_turn(n)
                if g == 1 and not is_first:
                    out_project(d)
                if g == 2 and not is_last:
                    ak(n)
                if g == 3 and not is_last:
                    avp(n)
                if g == 5 and not is_last:
                    x_turn(n)
                if g == 6 and not is_last:
                    q(n)
            if not is_first:
                h_turn(d)
            if not is_last:
                k(n)
            max_turn(b)
            if not is_first:
                router(d)
            for u in range(2 * GROUPS):
                if u == 6 and not is_first:
                    places(d)
                if u == 5 and not is_last:
                    v(n)
                scores_T(b, u // 2, u % 2)
                if u:
                    values(b, (u - 1) // 2, (u - 1) % 2)
            values(b, GROUPS - 1, 1)

        def first(n):
            pe.wait_ge(dve_c.sem, 1)
            ctx_turn(n)
            wait_weight(1)
            ak(n)
            wait_weight(2)
            avp(n)
            x_turn(n)
            wait_weight(3)
            q(n)
            k(n)
            v(n)
            wait_weight(4)
            pe.wait_ge(dve_c.sem, 4)

        def last(n):
            out_turn(n)
            out_project(n)
            h_turn(n)
            router(n)
            places(n)

        walk(pe, step, first, last)


def expert_phase(nc, ctx, dram, keep):
    def sb(name, shape, dt):
        return ctx.enter_context(nc.sbuf_tensor(name, shape, dt))

    def ps(name, shape, dt):
        return ctx.enter_context(nc.psum_tensor(name, shape, dt))

    def sem(name):
        return ctx.enter_context(nc.semaphore(name))

    def ev(name, per=1):
        return Event(sem(name), per)

    w1s, count, ident16, held = keep["w1s"], keep["count"], keep["ident16"], keep["held"]
    KF = len(FCH)
    LB = 4

    w2f = [sb(f"w2f{k}", [P, KF, D], F32) for k in range(2)]
    w2s = sb("w2s", [P, NE, KF, 2, D], F16)
    iot = sb("iot", [P, SLOTS], I32)
    slot = sb("slot", [P, SLOTS], F32)
    steps = sb("steps", [P, NE, T // P], F32)
    tiles = sb("tiles", [P, NE], F32)
    ends = sb("ends", [P, NE], F32)
    past = sb("past", [P, SLOTS, NE], F32)
    past2 = sb("past2", [P, SLOTS, NE], F32)
    ex = sb("ex", [P, SLOTS], F32)
    begin = sb("begin", [P, SLOTS], F32)
    valid = sb("valid", [P, SLOTS], F32)
    at = sb("at", [P, SLOTS], F32)
    exi = sb("exi", [P, SLOTS], I32)
    ati = sb("ati", [P, SLOTS], I32)
    lrow = sb("lrow", [P, LB, 2], F32)
    wrow = sb("wrow", [P, 2], F32)
    hg = sb("hg", [P, 2, 2, D], F16)
    hgT = sb("hgT", [P, 2, 2, NC_, P], F16)
    sg = sb("sg", [P, F], F32)
    ya = sb("ya", [P, F], F32)
    yp = sb("yp", [P, 2, F], F16)
    yT = sb("yT", [P, 2, KF, P], F16)
    yo = sb("yo", [P, 2, D], F32)

    y1 = [[ps(f"y1_{k}{j}", [P, 512], F32) for j in range(2)] for k in range(2)]
    px = ps("px", [P, 8, P], F16)
    py = ps("py", [P, 8, P], F16)
    y2 = [ps(f"y2_{k}", [P, 512], F32) for k in range(2)]

    w2_in = [sem(f"w2_in{k}") for k in range(2)]
    w2_hi, w2_lo = ev("w2_hi"), ev("w2_lo")
    tab, iot_d = ev("tab"), ev("iot_d")
    l_in = Loaded([sem(f"l_in{k}") for k in range(LB)])
    g_in = Loaded([sem(f"g_in{k}") for k in range(2)])
    added = Loaded([sem("added")])
    gather_held, add_held = ev("gather_held"), ev("add_held")
    w_row, g_tp, g_T, gate_p, up_p, g_silu, y_a, y_hi, y_lo, y_tp, y_T, y_p, y_o = (
        ev(n) for n in ("w_row", "g_tp", "g_T", "gate_p", "up_p", "g_silu", "y_a", "y_hi", "y_lo", "y_tp",
                        "y_T", "y_p", "y_o"))
    TAB = 16

    block = ctx.enter_context(nc.Block())

    def number(eng, table, n, top):
        return eng.value_load(table[0:1, bass.ds(n.n, 1)], min_val=0, max_val=top)

    def walk(eng, step):
        head = (SLOTS - 1) % LB + LB
        for k in range(head):
            step(Batch(0, k, LB), k == 0, False)
        with eng.Fori(0, (SLOTS - 1 - head) // LB) as it:
            for k in range(LB):
                step(Batch(it, head + k, LB), False, False)
        step(Batch(0, SLOTS - 1, LB), False, True)

    @block.sync
    def _(sp):
        for e in range(NE):
            if e >= 2:
                sp.wait_ge(w2_lo.sem, w2_lo.at(Batch(0, 0), 2 * (e - 1)))
            for k, (f0, fn) in enumerate(FCH[1:]):
                if k == 0:
                    sp.dma_start(w2f[e % 2][:, 0:2, :], dram["w2a"][e]).then_inc(w2_in[e % 2], 16)
                else:
                    sp.dma_start(w2f[e % 2][0:fn, 2, :], dram["w2b"][e]).then_inc(w2_in[e % 2], 16)
        sp.wait_ge(tab.sem, tab.at(Batch(0, 0), TAB))

        def step(s, is_first, is_last):
            place = number(sp, ati, s, NE * (T // P) - 1)
            sp.wait_ge(added.sem(s), added.at(s.shift(-LB)))
            sp.dma_start(lrow[:, s.off % LB, :], dram["list_tiles"][bass.ds(place, 1), :, :].rearrange(
                "a p n -> (a p) n")).then_inc(l_in.sem(s), 16)

        walk(sp, step)

    @block.gpsimd
    def _(pool):
        pool.iota(iot[:, :], pattern=[[1, SLOTS]], base=0, channel_multiplier=0).then_inc(iot_d.sem, 1)

        def gather(s):
            pool.wait_ge(l_in.sem(s), l_in.at(s))
            pool.wait_ge(g_tp.sem, g_tp.at(s.shift(-2)))
            pool.wait_ge(gather_held.sem, gather_held.at(s.shift(-1)))
            pool.tensor_tensor(held[:, 0:1], held[:, 2:3], held[:, 2:3], ALU.add).then_inc(gather_held.sem, 1)
            pool.indirect_dma_start(
                out=hg[:, s.par, :, :].rearrange("p a n -> p (a n)"), out_offset=None, in_=dram["h2_rows"],
                in_offset=bass.IndirectOffsetOnAxis(ap=lrow[:, s.off % LB, 0:1].bitcast(I32), axis=0)
            ).then_inc(g_in.sem(s), 16)

        def add(s):
            pool.wait_ge(y_o.sem, y_o.at(s))
            pool.wait_ge(added.sem(s), added.at(s.shift(-1)))
            pool.wait_ge(add_held.sem, add_held.at(s.shift(-1)))
            pool.tensor_tensor(held[:, 1:2], held[:, 2:3], held[:, 2:3], ALU.add).then_inc(add_held.sem, 1)
            pool.indirect_dma_start(
                out=dram["out_rows"], out_offset=bass.IndirectOffsetOnAxis(
                    ap=lrow[:, s.off % LB, 0:1].bitcast(I32), axis=0),
                in_=yo[:, s.par, :], in_offset=None, compute_op=ALU.add).then_inc(added.sem(s), 16)

        def step(s, is_first, is_last):
            gather(s)
            if s.off >= 2:
                add(s.shift(-2))
            if is_last:
                add(s.shift(-1))
                add(s)

        walk(pool, step)
        pool.wait_ge(added.sem(Batch(0, SLOTS - 1, LB)), added.at(Batch(0, SLOTS - 1, LB)))

    @block.scalar
    def _(act):
        for e in range(NE):
            act.wait_ge(w2_in[e % 2], 32 * (e // 2) + 32)
            act.activation(w2s[:, e, 0:2, 0, :], w2f[e % 2][:, 0:2, :], ACT.Copy, scale=WS).then_inc(w2_hi.sem, 1)
            act.activation(w2s[0:96, e, 2, 0, :], w2f[e % 2][0:96, 2, :], ACT.Copy, scale=WS).then_inc(w2_hi.sem, 1)

        def step(s, is_first, is_last):
            d = s.shift(-1)
            act.wait_ge(g_tp.sem, g_tp.at(s))
            act.wait_ge(up_p.sem, up_p.at(s.shift(-2)))
            act.activation(hgT[:, s.par, :, :, :].rearrange("p a c n -> p (a c) n"), px[:, :, :],
                           ACT.Copy).then_inc(g_T.sem, 1)
            if not is_first:
                expert_out(d)
            act.wait_ge(gate_p.sem, gate_p.at(s))
            act.wait_ge(y_a.sem, y_a.at(s.shift(-1)))
            act.activation(sg[:, :], y1[s.par][0][:, 0:F], ACT.Silu, scale=1 / WS).then_inc(g_silu.sem, 1)
            act.wait_ge(y_a.sem, y_a.at(s))
            act.wait_ge(y_tp.sem, y_tp.at(s.shift(-1)))
            act.activation(yp[:, 0, :], ya[:, :], ACT.Copy).then_inc(y_hi.sem, 1)
            if is_last:
                expert_out(s)

        def expert_out(s):
            act.wait_ge(y_p.sem, y_p.at(s))
            act.wait_ge(w_row.sem, w_row.at(s))
            act.wait_ge(added.sem(s), added.at(s.shift(-2)))
            act.activation(yo[:, s.par, :], y2[s.par][:, :], ACT.Copy, scale=wrow[:, s.par:s.par + 1]
                           ).then_inc(y_o.sem, 1)

        walk(act, step)

    @block.vector
    def _(dve):
        made = [0]

        def table(ins):
            ins.then_inc(tab.sem, 1)
            made[0] += 1
            dve.wait_ge(tab.sem, made[0])

        dve.wait_ge(iot_d.sem, iot_d.at(Batch(0, 0)))
        table(dve.tensor_copy(slot[:, :], iot[:, :]))
        table(dve.tensor_scalar(steps[:, 0, :], slot[:, 0:T // P], float(P), None, ALU.mult))
        table(dve.tensor_copy(steps[:, 1:NE, :], steps[:, 0:1, :].to_broadcast([P, NE - 1, T // P])))
        table(dve.tensor_tensor(steps[:, :, :], count[:, :].unsqueeze(2).to_broadcast([P, NE, T // P]),
                                steps[:, :, :], ALU.is_gt))
        table(dve.tensor_reduce(tiles[:, :], steps[:, :, :], AX.X, ALU.add))
        table(dve.tensor_tensor_scan(ends[:, :], tiles[:, :], tiles[:, :], 0.0, ALU.add, ALU.bypass))
        table(dve.tensor_tensor(past[:, :, :], ends[:, :].unsqueeze(1).to_broadcast([P, SLOTS, NE]),
                                slot[:, :].unsqueeze(2).to_broadcast([P, SLOTS, NE]), ALU.is_le))
        table(dve.tensor_tensor(past2[:, :, :], past[:, :, :],
                                tiles[:, :].unsqueeze(1).to_broadcast([P, SLOTS, NE]), ALU.mult))
        table(dve.tensor_reduce(ex[:, :], past[:, :, :], AX.X, ALU.add))
        table(dve.tensor_reduce(begin[:, :], past2[:, :, :], AX.X, ALU.add))
        table(dve.tensor_scalar(valid[:, :], ex[:, :], float(NE), None, ALU.is_lt))
        table(dve.tensor_tensor(ex[:, :], ex[:, :], valid[:, :], ALU.mult))
        table(dve.tensor_tensor(at[:, :], slot[:, :], begin[:, :], ALU.subtract))
        table(dve.scalar_tensor_tensor(out=at[:, :], in0=ex[:, :], scalar=float(T // P), in1=at[:, :],
                                       op0=ALU.mult, op1=ALU.add))
        table(dve.tensor_copy(exi[:, :], ex[:, :]))
        table(dve.tensor_tensor(ati[:, :], at[:, :], valid[:, :], ALU.mult))
        assert made[0] == TAB
        for e in range(NE):
            dve.wait_ge(w2_hi.sem, w2_hi.at(Batch(0, 0), 2 * e + 2))
            dve.scalar_tensor_tensor(out=w2s[:, e, 0:2, 1, :], in0=w2f[e % 2][:, 0:2, :], scalar=WS,
                                     in1=w2s[:, e, 0:2, 0, :], op0=ALU.mult, op1=ALU.subtract).then_inc(w2_lo.sem, 1)
            dve.scalar_tensor_tensor(out=w2s[0:96, e, 2, 1, :], in0=w2f[e % 2][0:96, 2, :], scalar=WS,
                                     in1=w2s[0:96, e, 2, 0, :], op0=ALU.mult, op1=ALU.subtract).then_inc(w2_lo.sem, 1)

        def step(s, is_first, is_last):
            dve.wait_ge(l_in.sem(s), l_in.at(s))
            dve.wait_ge(y_o.sem, y_o.at(s.shift(-2)))
            dve.scalar_tensor_tensor(out=wrow[:, s.par:s.par + 1], in0=lrow[:, s.off % LB, 1:2],
                                     scalar=1 / (WS * YS), in1=valid[:, bass.ds(s.n, 1)],
                                     op0=ALU.mult, op1=ALU.mult).then_inc(w_row.sem, 1)
            dve.wait_ge(g_silu.sem, g_silu.at(s))
            dve.wait_ge(up_p.sem, up_p.at(s))
            dve.wait_ge(y_lo.sem, y_lo.at(s.shift(-1)))
            dve.wait_ge(y_hi.sem, y_hi.at(s.shift(-1)))
            dve.scalar_tensor_tensor(out=ya[:, :], in0=y1[s.par][1][:, 0:F], scalar=YS / WS, in1=sg[:, :],
                                     op0=ALU.mult, op1=ALU.mult).then_inc(y_a.sem, 1)
            dve.wait_ge(y_hi.sem, y_hi.at(s))
            dve.tensor_tensor(yp[:, 1, :], ya[:, :], yp[:, 0, :], ALU.subtract).then_inc(y_lo.sem, 1)
            dve.wait_ge(y_tp.sem, y_tp.at(s))
            dve.wait_ge(y_p.sem, y_p.at(s.shift(-1)))
            for part in range(2):
                dve.tensor_copy(yT[:, part, 0:2, :], py[:, KF * part:KF * part + 2, :])
                i = dve.tensor_copy(yT[0:96, part, 2, :], py[0:96, KF * part + 2, :])
            i.then_inc(y_T.sem, 1)

        walk(dve, step)

    @block.tensor
    def _(pe):
        def turn_rows(s):
            pe.wait_ge(g_in.sem(s), g_in.at(s))
            pe.wait_ge(g_T.sem, g_T.at(s.shift(-1)))
            for part in range(2):
                for c in range(NC_):
                    i = pe.transpose(px[:, part * NC_ + c, :], hg[:, s.par, part, c * P:(c + 1) * P], ident16[:, :])
            i.then_inc(g_tp.sem, 1)

        def inner(s, j, e):
            if j == 0:
                pe.wait_ge(g_T.sem, g_T.at(s))
            n = 0
            for a, z in TERMS:
                for c in range(NC_):
                    w = w1s[:, bass.ds(e * NC_ + c, 1), z, j * F:(j + 1) * F].rearrange("p a n -> p (a n)")
                    i = pe.matmul(y1[s.par][j][:, 0:F], hgT[:, s.par, a, c, :], w, start=(n == 0), stop=(n == 11))
                    n += 1
            i.then_inc((gate_p, up_p)[j].sem, 1)

        def turn_inner(s):
            pe.wait_ge(y_hi.sem, y_hi.at(s))
            pe.wait_ge(y_lo.sem, y_lo.at(s))
            for part in range(2):
                for k, (f0, fn) in enumerate(FCH):
                    i = pe.transpose(py[0:fn, KF * part + k, :], yp[:, part, f0:f0 + fn], ident16[:, :])
            i.then_inc(y_tp.sem, 1)

        def outer(s, e):
            pe.wait_ge(y_T.sem, y_T.at(s))
            pe.wait_ge(y_o.sem, y_o.at(s.shift(-2)))
            n = 0
            for a, z in TERMS:
                for k, (f0, fn) in enumerate(FCH):
                    w = w2s[0:fn, bass.ds(e, 1), k, z, :].rearrange("p a n -> p (a n)")
                    i = pe.matmul(y2[s.par][:, :], yT[0:fn, a, k, :], w, start=(n == 0), stop=(n == 8))
                    n += 1
            i.then_inc(y_p.sem, 1)

        pe.wait_ge(tab.sem, tab.at(Batch(0, 0), TAB))

        def step(s, is_first, is_last):
            d = s.shift(-1)
            if is_first:
                turn_rows(s)
            e = number(pe, exi, s, NE - 1)
            inner(s, 0, e)
            if not is_first:
                turn_inner(d)
            inner(s, 1, e)
            if not is_last:
                turn_rows(s.shift(1))
            if is_first:
                pe.wait_ge(w2_lo.sem, w2_lo.at(Batch(0, 0), 2 * NE))
                pe.wait_ge(w2_hi.sem, w2_hi.at(Batch(0, 0), 2 * NE))
            else:
                outer(d, number(pe, exi, d, NE - 1))
            if is_last:
                turn_inner(s)
                outer(s, number(pe, exi, s, NE - 1))

        walk(pe, step)


def program(nc, x, ctx, mask, wq, wk, wv, wo, gate, router, w1, w2a, w2b, rope, out):
    def tile(t):
        return lambda n: t[bass.ds(n.n, 1), :, :].rearrange("a p n -> (a p) n")

    h2 = nc.dram_tensor("h2_pairs", [T, 2 * D], F16, kind="Internal").ap()
    lists = nc.dram_tensor("lists", [NE * T, 2], F32, kind="Internal").ap()
    with ExitStack() as both:
        w1s = both.enter_context(nc.sbuf_tensor("w1s", [P, NE * NC_, 2, 2 * F], F16))
        count = both.enter_context(nc.sbuf_tensor("count", [P, NE], F32))
        ident16 = both.enter_context(nc.sbuf_tensor("ident16", [P, P], F16))
        held = both.enter_context(nc.sbuf_tensor("held", [P, 4], F32))

        def stage(n):
            room = w1s[:, 20:32, :, :].rearrange("p s a n -> p (s a n)").bitcast(F32)
            return room[:, n * NC_ * D:(n + 1) * NC_ * D].rearrange("p (c n) -> p c n", c=NC_)

        keep = dict(w1s=w1s, count=count, ident16=ident16, stage=stage, held=held)
        with ExitStack() as stack:
            attention_phase(nc, stack, dict(
                x=tile(x), ctx=tile(ctx), mask=tile(mask), w=(wq, wk, wv, wo), gate=gate, router=router,
                w1=tile(w1), rope=rope, out=tile(out), h2=tile(h2.rearrange("(b p) n -> b p n", p=P)),
                lists=lists), keep)
        with ExitStack() as stack:
            expert_phase(nc, stack, dict(
                w2a=w2a, w2b=w2b, h2_rows=h2, list_tiles=lists.rearrange("(t p) n -> t p n", p=P),
                out_rows=out.rearrange("b p n -> (b p) n")), keep)


def rope_tables():
    inv = 1.0 / 10000.0 ** (np.arange(0, HD, 2, dtype=np.float32) / HD)
    freqs = np.outer(np.arange(P, dtype=np.float32), inv)
    cos, sin = np.cos(freqs).astype(np.float32), np.sin(freqs).astype(np.float32)
    cos, sin = np.concatenate([cos, cos], 1), np.concatenate([-sin, sin], 1)
    q, k = np.float32(HD ** -0.5 / WS), np.float32(1 / WS)
    return np.stack([cos * q, sin * q, cos * k, sin * k], 1)


def kernel(x, ctx_2048, mask_Bx1xSxS_fk0, L0_xattn_Wq, L0_xattn_Wk, L0_xattn_Wv, L0_xattn_Wo, L0_xattn_gate,
           L0_ffn_router_w, L0_ffn_w1, L0_ffn_w2):
    import concourse.bacc as bacc
    from concourse.bass_utils import run_bass_kernel_spmd

    def chunks(w):
        return np.ascontiguousarray(np.asarray(w).reshape(NC_, P, -1).transpose(1, 0, 2))

    w1 = np.asarray(L0_ffn_w1).transpose(0, 2, 1).reshape(NE * NC_, P, 2 * F)
    w2 = np.asarray(L0_ffn_w2).transpose(0, 2, 1)
    arrays = {
        "x": np.asarray(x), "ctx": np.asarray(ctx_2048), "mask": np.asarray(mask_Bx1xSxS_fk0).reshape(NB, P, P),
        "wq": chunks(L0_xattn_Wq), "wk": chunks(L0_xattn_Wk), "wv": chunks(L0_xattn_Wv), "wo": chunks(L0_xattn_Wo),
        "gate": np.asarray(L0_xattn_gate).reshape(1, NH), "router": chunks(np.asarray(L0_ffn_router_w).T),
        "w1": w1, "w2a": w2[:, 0:2 * P].reshape(NE, 2, P, D).transpose(0, 2, 1, 3), "w2b": w2[:, 2 * P:],
        "rope": rope_tables(),
    }
    arrays = {f"in_{n}": np.ascontiguousarray(a) for n, a in arrays.items()}
    nc = bacc.Bacc("TRN2", target_bir_lowering=False, num_devices=1)
    args = [nc.dram_tensor(n, a.shape, mybir.dt.from_np(a.dtype), kind="ExternalInput").ap()
            for n, a in arrays.items()]
    out = nc.dram_tensor("out", (NB, P, D), F32, kind="ExternalOutput").ap()
    program(nc, *args, out)
    r = run_bass_kernel_spmd(nc, [arrays], core_ids=[0])
    return r.results[0]["out"]
```

```python
from contextlib import ExitStack

import numpy as np

import concourse.bass as bass
from concourse import mybir

F32, F32R, F16 = mybir.dt.float32, mybir.dt.float32r, mybir.dt.float16
BF16, I32, U32 = mybir.dt.bfloat16, mybir.dt.int32, mybir.dt.uint32
ALU, ACT, AX = mybir.AluOpType, mybir.ActivationFunctionType, mybir.AxisListType

P = 128
NB = 32
T = NB * P
D = 512
NC_ = D // P
NH = 32
HD = D // NH
NE = 8
F = 352
FCH = [(0, 128), (128, 128), (256, 96)]
WS = 64.0
YS = 16.0
EPS = 1e-5
PAIRS = NH // 2
GROUPS = NH // 4
VW = HD + 1
LB = 4
SLOTS = 2 * T // P + NE - 1
TAB = 16
TERMS = ((0, 0), (0, 1), (1, 0))


class Batch:

    def __init__(self, it, off, unroll=2):
        self.it, self.off, self.unroll = it, off, unroll
        self.n = unroll * it + off
        self.par = off % 2

    def shift(self, d):
        return Batch(self.it, self.off + d, self.unroll)

    def use(self, buffers):
        return self.unroll // buffers * self.it + self.off // buffers


class Event:

    def __init__(self, sem, per=1):
        self.sem, self.per = sem, per

    def at(self, batch, k=None):
        value = self.per * batch.n + (self.per if k is None else k)
        return max(value, 0) if isinstance(value, int) else value


class Loaded:

    def __init__(self, sems):
        self.sems = sems

    def sem(self, batch):
        return self.sems[batch.off % len(self.sems)]

    def at(self, batch):
        value = 16 * batch.use(len(self.sems)) + 16
        return max(value, 0) if isinstance(value, int) else value


def attention_phase(nc, ctx, dram, keep):
    def sb(name, shape, dt):
        return ctx.enter_context(nc.sbuf_tensor(name, shape, dt))

    def ps(name, shape, dt):
        return ctx.enter_context(nc.psum_tensor(name, shape, dt))

    def ev(name, per=1):
        return Event(keep["semaphores"].enter_context(nc.semaphore(name)), per)

    def ld(name, n):
        return Loaded([keep["semaphores"].enter_context(nc.semaphore(f"{name}{k}")) for k in range(n)])

    w1s, count, ident16, held = keep["w1s"], keep["count"], keep["ident16"], keep["held"]
    entry, tab = keep["entry"], keep["tab"]
    wst = keep["wst"]
    iot, slot, tiles, ends, ex, begin, valid, at, exi, ati = keep["slots"]

    wts = keep["qkv"] + [sb("w_o", [P, NC_, 2, D], F16)]
    wq, wk, wv, wo = wts
    identr = sb("identr", [P, P], F32R)
    identf = sb("identf", [P, P], F32)
    ident_bf = sb("ident_bf", [P, P], BF16)
    tri = sb("tri", [P, P], BF16)
    ones = sb("ones", [P, P], BF16)
    hsel = sb("hsel", [3 * NH, NH], BF16)
    rope = sb("rope", [P, 4, HD], F32)
    tg = sb("tg", [P, NH], F32)
    xin = sb("xin", [P, 2, D], F32)
    xres = sb("xres", [P, 2, D], F32)
    cin = sb("cin", [P, D], F32)
    msk = sb("msk", [P, 2, P], F32)
    mskp = sb("mskp", [P, 2, 2, P], F32R)
    stat = sb("stat", [P, 2, 8], F32)
    mv = sb("mv", [P, 2, 4], F32)
    mhalf = sb("mhalf", [P, 1], F32)
    scale = sb("scale", [P, 1], F32)
    xcs = sb("xcs", [P, 2, D], F16)
    xT = sb("xT", [P, 2, NC_, P], F16)
    cT = sb("cT", [P, 2, NC_, P], F16)
    t1 = sb("t1", [P, D], F32)
    t2 = sb("t2", [P, D], F32)
    qs = sb("qs", [P, NH, 4, HD], F16)
    ks = sb("ks", [P, NH, 4, HD], F16)
    aks = sb("aks", [P, NH, 4, HD], F16)
    qz = sb("qz", [P, PAIRS, 2, P], F16)
    kk = sb("kk", [P, 2, PAIRS, P], F16)
    kst, akst = kk[:, 0], kk[:, 1]
    vv = sb("vv", [P, 2, 2, NH, VW], F32)
    mx = sb("mx", [P, 2, NH], F32)
    mr = sb("mr", [P, 2, NH], F32)
    mp = sb("mp", [P, 2, 3, NH], BF16)
    mT = sb("mT", [3 * NH, 2, P], BF16)
    pr = sb("pr", [P, 2, 4, P], F32)
    avs = sb("avs", [P, NH, 2, VW], F32)
    rc = sb("rc", [P, NH, 2], F32)
    nat = sb("nat", [P, D], F32)
    oT = sb("oT", [P, 2, NC_, P], F16)
    x2 = sb("x2", [P, D], F32)
    ohs = sb("ohs", [P, 2, D], F16)
    hT = sb("hT", [P, 2, NC_, P], F16)
    rwf = sb("rwf", [P, NC_, NE], F32)
    rw = sb("rw", [P, NC_, 2, NE], F16)
    lg = sb("lg", [P, NE], F32)
    top = sb("top", [P, 8], F32)
    key = sb("key", [P, 2, NE], F32)
    lowest = sb("lowest", [P, 2], F32)
    gap = sb("gap", [P, 4], F32)
    w2nd = sb("w2nd", [P, 1], F32)
    iota8 = sb("iota8", [P, NE], F32)
    ebase = sb("ebase", [P, NE], F32)
    oh = sb("oh", [P, 2, NE], F32)
    sel = sb("sel", [P, NE], BF16)
    unsel = sb("unsel", [P, NE], F32)
    wsel = sb("wsel", [P, NE], F32)
    tok = sb("tok", [P, 2], F32)
    pos = sb("pos", [P, NE], F32)
    posi = sb("posi", [P, NE], I32)
    row = sb("row", [P, NE, 2], F32)

    st = [ps(f"st{k}", [P, 4, P], F32) for k in range(2)]
    av = [ps(f"av{k}", [P, 8, 2, VW], F32) for k in range(2)]
    ma = [ps(f"ma{k}", [P, 512], F32) for k in range(2)]
    md = [ps(f"md{k}", [P, 512], F32) for k in range(2)]
    sm = [bank[:, :].rearrange("p (a n) -> p a n", a=4) for bank in md]

    def half(bank):
        return bank[:, :].bitcast(F16).rearrange("p (a n) -> p a n", a=8)

    x_in, c_in, m_in, w_in = ld("x_in", 2), ld("c_in", 1), ld("m_in", 2), ld("w_in", 1)
    out_st, h2_st = ld("out_st", 1), ld("h2_st", 1)
    list_st, list_held = ev("list_st", 16 * NE), ev("list_held")
    const_in, wt_in = ld("const_in", 1), [ld(f"wt_in{k}", 1) for k in range(4)]
    pool_c, dve_c, act_c = ev("pool_c"), ev("dve_c"), ev("act_c")
    iot_d = ev("iot_d")
    wt_hi, wt_lo = ev("wt_hi"), ev("wt_lo")
    x_part = ev("x_part", 2)
    x_ve, x_rs, x_kept, x_n = (ev(n) for n in ("x_ve", "x_rs", "x_kept", "x_n"))
    x_hi, x_lo, x_tp, x_T = ev("x_hi"), ev("x_lo"), ev("x_tp"), ev("x_T")
    c_hi, c_lo, c_tp, c_T = ev("c_hi"), ev("c_lo"), ev("c_tp"), ev("c_T")
    ak_p, av_p, q_p, k_p, v_p = (ev(n) for n in ("ak_p", "av_p", "q_p", "k_p", "v_p"))
    ak_hi, ak_lo, av_v, v_v = ev("ak_hi"), ev("ak_lo"), ev("av_v"), ev("v_v")
    q_t1, q_t2, q_r, q_hi, q_lo = (ev(n) for n in ("q_t1", "q_t2", "q_r", "q_hi", "q_lo"))
    k_t1, k_t2, k_r, k_hi, k_lo = (ev(n) for n in ("k_t1", "k_t2", "k_r", "k_hi", "k_lo"))
    m_hi, m_lo = ev("m_hi"), ev("m_lo")
    w_sc, w_hi, w_lo = ev("w_sc"), ev("w_hi"), ev("w_lo")
    stk_t, stk_o = ev("stk_t", GROUPS), ev("stk_o", GROUPS)
    s_pe, s_ad, s_own = ev("s_pe", GROUPS), ev("s_ad", GROUPS), ev("s_own", GROUPS)
    m_part, mp3, mp_t, m_T = ev("m_part", 4), ev("mp3"), ev("mp_t"), ev("m_T")
    t_pe, p_ex, av_pe, av_s = ev("t_pe", 2 * GROUPS), ev("p_ex", 2 * GROUPS), ev("av_pe", 2 * GROUPS), ev("av_s", 4)
    n_rc, n_rg, n_o1, n_o2, n_o = (ev(n) for n in ("n_rc", "n_rg", "n_o1", "n_o2", "n_o"))
    o_hi, o_lo, o_tp, o_T, o_p, x_2 = (ev(n) for n in ("o_hi", "o_lo", "o_tp", "o_T", "o_p", "x_2"))
    h_part = ev("h_part", 2)
    h_ve, h_rs, h_n, h_hi, h_lo = (ev(n) for n in ("h_ve", "h_rs", "h_n", "h_hi", "h_lo"))
    h_tp, h_T, r_p, r_lg = (ev(n) for n in ("h_tp", "h_T", "r_p", "r_lg"))
    r_pick = ev("r_pick", 10)
    r_gap, r_ex, r_weigh = ev("r_gap"), ev("r_ex"), ev("r_weigh", 4)
    r_sel, r_un, r_row = (ev(n) for n in ("r_sel", "r_un", "r_row"))
    f_p, f_c, f_pos, f_cnt, f_step = ev("f_p"), ev("f_c"), ev("f_pos"), ev("f_cnt"), ev("f_step", 4)

    block = ctx.enter_context(nc.Block())
    A0 = Batch(0, 0)

    def walk(eng, step, first, last):
        def near(b, lacks):
            step(b, *(None if d in lacks else b.shift(d) for d in (-2, -1, 1, 2)))

        first(Batch(0, 0))
        near(Batch(0, 0), (-2, -1))
        near(Batch(0, 1), (-2,))
        near(Batch(0, 2), ())
        near(Batch(0, 3), ())
        with eng.Fori(0, NB // 2 - 3) as it:
            near(Batch(it, 4), ())
            near(Batch(it, 5), ())
        near(Batch(0, NB - 2), (2,))
        near(Batch(0, NB - 1), (1, 2))
        last(Batch(0, NB - 1))

    def heads(t):
        return t[:, :].rearrange("p (h d) -> p h d", d=HD)

    def twice(t):
        return heads(t).unsqueeze(2).to_broadcast([P, NH, 2, HD])

    def slice_of(n, part):
        return w1s[:, bass.ds(n.n, 1), part, :].rearrange("p a n -> p (a n)")

    def m_bank():
        return md[0][:, :].bitcast(BF16)[:, 0:2 * P].rearrange(
            "p (a n) -> p a n", a=2)

    @block.sync
    def _(sp):
        def load_x(n):
            source = dram["x"](n)
            sp.wait_ge(x_kept.sem, x_kept.at(n.shift(-2)))
            sp.wait_ge(x_n.sem, x_n.at(n.shift(-2)))
            sp.dma_start(xin[:, n.par, :], source).then_inc(x_in.sem(n), 16)

        def load_c(n):
            source = dram["ctx"](n)
            sp.wait_ge(c_lo.sem, c_lo.at(n.shift(-1)))
            sp.dma_start(cin[:, :], source).then_inc(c_in.sem(n), 16)

        def load_m(n):
            source = dram["mask"](n)
            sp.wait_ge(m_lo.sem, m_lo.at(n.shift(-2)))
            sp.wait_ge(s_own.sem, s_own.at(n.shift(-2)))
            sp.dma_start(msk[:, n.par, :], source).then_inc(m_in.sem(n), 16)

        def load_w(n):
            source = dram["w1"](n)
            sp.wait_ge(w_lo.sem, w_lo.at(n.shift(-1)))
            sp.dma_start(wst[:, :], source).then_inc(w_in.sem(n), 16)

        def store(n):
            out, h2 = dram["out"](n), dram["h2"](n)
            sp.wait_ge(x_2.sem, x_2.at(n))
            sp.dma_start(out, x2[:, :]).then_inc(out_st.sem(n), 16)
            sp.wait_ge(h_lo.sem, h_lo.at(n))
            sp.wait_ge(h_hi.sem, h_hi.at(n))
            sp.dma_start(h2, ohs[:, :, :].rearrange("p a n -> p (a n)")).then_inc(h2_st.sem(n), 16)

        for k, n in enumerate((0, 1, 2, 3)):
            stage = keep["stage"](n)
            sp.dma_start(stage, dram["w"][n]).then_inc(wt_in[n].sems[0], 16)
            if k == 0:
                load_c(A0)
                load_x(A0)
                load_m(A0)
                sp.dma_start(rope[:, :, :], dram["rope"]).then_inc(const_in.sems[0], 16)
                sp.dma_start(tg[:, :], dram["gate"].to_broadcast([P, NH])).then_inc(const_in.sems[0], 16)
                sp.dma_start(rwf[:, :, :], dram["router"]).then_inc(const_in.sems[0], 16)
        load_w(A0)

        load_x(A0.shift(1))

        def step(b, c, d, n, m):
            if m:
                load_x(m)
            if n:
                load_c(n)
                load_m(n)
            if d:
                store(d)
            if n:
                load_w(n)

        def last(n):
            for used in (v_p, av_p):
                sp.wait_ge(used.sem, used.at(n))
            for e in range(len(keep["w2f"])):
                sp.dma_start(keep["w2f"][e][:, 0:2, :], dram["w2a"][e]).then_inc(keep["w2_in"][e], 16)
                sp.dma_start(keep["w2f"][e][0:96, 2, :], dram["w2b"][e]).then_inc(keep["w2_in"][e], 16)
            store(n)

        walk(sp, step, lambda b: None, last)
        sp.wait_ge(out_st.sem(Batch(0, NB - 1)), out_st.at(Batch(0, NB - 1)))
        sp.wait_ge(h2_st.sem(Batch(0, NB - 1)), h2_st.at(Batch(0, NB - 1)))

    @block.gpsimd
    def _(pool):
        marks = [0]

        def const(ins):
            ins.then_inc(pool_c.sem, 1)
            marks[0] += 1
            pool.wait_ge(pool_c.sem, marks[0])

        const(pool.memset(mhalf[:, :], -0.5))
        const(pool.memset(held[:, 2:4], 1.0))
        const(pool.memset(scale[:, :], WS))
        const(pool.memset(identf[:, :], 1.0))
        const(pool.affine_select(out=identf[:, :], in_=identf[:, :], compare_op=ALU.is_equal, fill=0.0,
                                 base=0, pattern=[[-1, P]], channel_multiplier=1))
        const(pool.memset(vv[:, :, :, :, HD:VW], 1.0))
        const(pool.memset(qz[:, :, :, :], 0.0))
        const(pool.memset(ones[:, :], 1.0))
        const(pool.affine_select(out=tri[:, :], in_=ones[:, :], compare_op=ALU.is_gt, fill=0.0,
                                 base=0, pattern=[[1, P]], channel_multiplier=-1))
        const(pool.memset(hsel[:, :], 0.0))
        for part in range(3):
            const(pool.affine_select(out=hsel[:, :], in_=hsel[:, :], compare_op=ALU.not_equal, fill=1.0,
                                     base=-NH * part, pattern=[[-1, NH]], channel_multiplier=1))
        const(pool.iota(posi[:, 0:NE], pattern=[[1, NE]], base=0, channel_multiplier=0))
        const(pool.tensor_copy(iota8[:, :], posi[:, 0:NE]))
        const(pool.iota(posi[:, 0:1], pattern=[[1, 1]], base=0, channel_multiplier=1))
        const(pool.tensor_copy(tok[:, 0:1], posi[:, 0:1]))
        const(pool.tensor_scalar(tok[:, 1:2], tok[:, 0:1], -1.0, float(T - 1), ALU.mult, ALU.add))
        const(pool.tensor_scalar(ebase[:, :], iota8[:, :], float(T), None, ALU.mult))
        const(pool.memset(count[:, :], 0.0))

        def stage_a(n):
            pool.wait_ge(x_ve.sem, x_ve.at(n))
            pool.tensor_tensor(mv[:, 0, 3:4], mv[:, 0, 2:3], mhalf[:, :], ALU.pow).then_inc(x_rs.sem, 1)

        def x_low(n):
            pool.wait_ge(x_hi.sem, x_hi.at(n))
            pool.tensor_tensor(xcs[:, 1, :], nat[:, :], xcs[:, 0, :], ALU.subtract).then_inc(x_lo.sem, 1)

        def keep_x(n):
            pool.wait_ge(x_in.sem(n), x_in.at(n))
            pool.wait_ge(x_2.sem, x_2.at(n.shift(-2)))
            one = held[:, 2:3].to_broadcast([P, D])
            pool.tensor_tensor(xres[:, n.par, :], xin[:, n.par, :], one, ALU.mult).then_inc(x_kept.sem, 1)

        def rotate(n, e1, e2, er, eh, el, high, rest):
            pool.wait_ge(e1.sem, e1.at(n))
            pool.wait_ge(e2.sem, e2.at(n))
            pool.tensor_tensor(t1[:, :], t1[:, :], t2[:, :], ALU.add).then_inc(er.sem, 1)
            pool.wait_ge(eh.sem, eh.at(n))
            pool.wait_ge(er.sem, er.at(n))
            pool.tensor_tensor(rest, twice(t1), high, ALU.subtract).then_inc(el.sem, 1)

        def step(b, c, d, n, m):
            if d:
                own_out(d)
            w_slice(b)
            if n:
                rotate(n, q_t1, q_t2, q_r, q_hi, q_lo, qs[:, :, 0:2, :], qs[:, :, 2:4, :])
                rotate(n, k_t1, k_t2, k_r, k_hi, k_lo, ks[:, :, 0:4:2, :], ks[:, :, 1:4:2, :])
            if d:
                norm_h(d)
            if n:
                keep_x(n)
            if m:
                stage_a(m)
                x_low(m)
            if c:
                enter_lists(c)

        def w_slice(n):
            pool.wait_ge(w_in.sem(n), w_in.at(n))
            by = scale[:, :].to_broadcast([P, 2 * F])
            pool.tensor_tensor(wst[:, :], wst[:, :], by, ALU.mult).then_inc(w_sc.sem, 1)
            pool.wait_ge(w_hi.sem, w_hi.at(n))
            pool.wait_ge(w_sc.sem, w_sc.at(n))
            pool.tensor_tensor(slice_of(n, 1), wst[:, :], slice_of(n, 0),
                               ALU.subtract).then_inc(w_lo.sem, 1)

        def own_out(n):
            pool.wait_ge(n_rc.sem, n_rc.at(n))
            pool.tensor_tensor(avs[:, :, 0, 0:HD], avs[:, :, 0, 0:HD],
                               rc[:, :, 0:1].to_broadcast([P, NH, HD]), ALU.mult).then_inc(n_o1.sem, 1)

        def norm_h(n):
            pool.wait_ge(h_ve.sem, h_ve.at(n))
            pool.tensor_tensor(mv[:, 1, 3:4], mv[:, 1, 2:3], mhalf[:, :], ALU.pow).then_inc(h_rs.sem, 1)

        def enter_lists(n):
            pool.wait_ge(f_pos.sem, f_pos.at(n))
            pool.wait_ge(r_row.sem, r_row.at(n))
            pool.wait_ge(list_held.sem, list_held.at(n.shift(-1)))
            pool.tensor_tensor(held[:, 1:2], held[:, 2:3], held[:, 2:3], ALU.add).then_inc(list_held.sem, 1)
            for e in range(NE):
                pool.indirect_dma_start(
                    out=dram["lists"], out_offset=bass.IndirectOffsetOnAxis(ap=posi[:, e:e + 1], axis=0),
                    in_=row[:, e, :], in_offset=None).then_inc(list_st.sem, 16)

        def first(n):
            stage_a(n)
            keep_x(n)
            rotate(n, q_t1, q_t2, q_r, q_hi, q_lo, qs[:, :, 0:2, :], qs[:, :, 2:4, :])
            rotate(n, k_t1, k_t2, k_r, k_hi, k_lo, ks[:, :, 0:4:2, :], ks[:, :, 1:4:2, :])
            stage_a(n.shift(1))
            x_low(n.shift(1))

        def last(n):
            pool.wait_ge(w_lo.sem, w_lo.at(n))
            pool.iota(iot, pattern=[[1, SLOTS]], base=0, channel_multiplier=0).then_inc(iot_d.sem, 1)
            own_out(n)
            norm_h(n)
            enter_lists(n.shift(-1))
            enter_lists(n)

        walk(pool, step, first, last)
        pool.wait_ge(list_st.sem, list_st.at(Batch(0, NB - 1)))

    @block.scalar
    def _(act):
        def x_high(n):
            act.wait_ge(x_n.sem, x_n.at(n))
            act.wait_ge(c_tp.sem, c_tp.at(n.shift(-1)))
            act.activation(xcs[:, 0, :], nat[:, :], ACT.Copy).then_inc(x_hi.sem, 1)

        def ctx_hi(n):
            act.wait_ge(c_in.sem(n), c_in.at(n))
            act.wait_ge(x_tp.sem, x_tp.at(n))
            act.activation(xcs[:, 0, :], cin[:, :], ACT.Copy).then_inc(c_hi.sem, 1)

        act.wait_ge(const_in.sem(A0), const_in.at(A0.shift(2)))
        act.activation(tg[:, :], tg[:, :], ACT.Tanh).then_inc(act_c.sem, 1)
        for k, n in enumerate((0, 1, 2, 3)):
            act.wait_ge(wt_in[n].sem(A0), wt_in[n].at(A0))
            act.activation(wts[n][:, :, 0, :], keep["stage"](n), ACT.Copy, scale=WS).then_inc(wt_hi.sem, 1)
            if k == 0:
                x_high(A0)
        act.wait_ge(const_in.sem(A0), const_in.at(A0.shift(2)))
        act.activation(rw[:, :, 0, :], rwf[:, :, :], ACT.Copy, scale=WS).then_inc(act_c.sem, 1)

        def x_turned(n):
            act.wait_ge(x_tp.sem, x_tp.at(n))
            act.wait_ge(v_p.sem, v_p.at(n.shift(-1)))
            act.activation(xT[:, :, :, :].rearrange("p a c n -> p (a c) n"), half(ma[0]),
                           ACT.Copy).then_inc(x_T.sem, 1)

        def ctx_turned(n):
            act.wait_ge(c_tp.sem, c_tp.at(n))
            act.wait_ge(av_p.sem, av_p.at(n.shift(-1)))
            act.activation(cT[:, :, :, :].rearrange("p a c n -> p (a c) n"), half(ma[0]),
                           ACT.Copy).then_inc(c_T.sem, 1)

        def ak_high(n):
            act.wait_ge(ak_p.sem, ak_p.at(n))
            act.wait_ge(stk_t.sem, stk_t.at(n.shift(-1)))
            act.activation(aks[:, :, 0:4:2, :], twice(ma[1]), ACT.Copy, scale=1 / WS).then_inc(ak_hi.sem, 1)

        def adapter_values(n):
            act.wait_ge(av_p.sem, av_p.at(n))
            act.wait_ge(av_pe.sem, av_pe.at(n.shift(-2)))
            act.activation(vv[:, n.par, 1, :, 0:HD], heads(ma[1]), ACT.Copy, scale=1 / WS).then_inc(av_v.sem, 1)

        def mask_hi(n):
            act.wait_ge(m_in.sem(n), m_in.at(n))
            act.wait_ge(t_pe.sem, t_pe.at(n.shift(-2)))
            act.activation(mskp[:, n.par, 0, :], msk[:, n.par, :], ACT.Copy).then_inc(m_hi.sem, 1)

        def q_high(n):
            act.wait_ge(q_r.sem, q_r.at(n))
            act.wait_ge(stk_t.sem, stk_t.at(n.shift(-1)))
            act.activation(qs[:, :, 0:2, :], twice(t1), ACT.Copy).then_inc(q_hi.sem, 1)

        def k_high(n):
            act.wait_ge(k_r.sem, k_r.at(n))
            act.wait_ge(stk_t.sem, stk_t.at(n.shift(-1)))
            act.activation(ks[:, :, 0:4:2, :], twice(t1), ACT.Copy).then_inc(k_hi.sem, 1)

        def own_values(n):
            act.wait_ge(v_p.sem, v_p.at(n))
            act.wait_ge(av_pe.sem, av_pe.at(n.shift(-2)))
            act.activation(vv[:, n.par, 0, :, 0:HD], heads(ma[0]), ACT.Copy, scale=1 / WS).then_inc(v_v.sem, 1)

        def stack_out(n, g):
            act.wait_ge(t_pe.sem, t_pe.at(n.shift(-1), 2 * g + 2))
            act.wait_ge(stk_t.sem, stk_t.at(n, g + 1))
            bank, pairs = half(ma[g % 2]), slice(2 * g, 2 * g + 2)
            for j in range(2):
                r = slice(64 * j, 64 * j + 64)
                act.activation(qz[r, pairs, j, :], bank[r, 0:2], ACT.Copy)
            keys = bank[:, 2:6].rearrange("p (k a) n -> p k a n", k=2)
            act.activation(kk[:, :, pairs, :], keys, ACT.Copy).then_inc(stk_o.sem, 1)

        def exps(n, u):
            path = u % 2
            act.wait_ge(t_pe.sem, t_pe.at(n, u + 1))
            act.wait_ge(av_pe.sem, av_pe.at(n, u - 1))
            act.activation(pr[:, path, :, :], st[path][:, :, :], ACT.Exp).then_inc(p_ex.sem, 1)

        def w_slice(n):
            act.wait_ge(w_sc.sem, w_sc.at(n))
            act.activation(slice_of(n, 0), wst[:, :], ACT.Copy).then_inc(w_hi.sem, 1)

        def out_hi(n):
            act.wait_ge(n_o.sem, n_o.at(n))
            act.wait_ge(h_tp.sem, h_tp.at(n.shift(-1)))
            act.wait_ge(h2_st.sem(n.shift(-1)), h2_st.at(n.shift(-1)))
            act.activation(ohs[:, 0, :], nat[:, :], ACT.Copy).then_inc(o_hi.sem, 1)

        def out_T(n):
            act.wait_ge(o_tp.sem, o_tp.at(n))
            act.wait_ge(o_p.sem, o_p.at(n.shift(-1)))
            act.activation(oT[:, :, :, :].rearrange("p a c n -> p (a c) n"), half(md[0]),
                           ACT.Copy).then_inc(o_T.sem, 1)

        def h_high(n):
            act.wait_ge(h_n.sem, h_n.at(n))
            act.wait_ge(o_tp.sem, o_tp.at(n))
            act.activation(ohs[:, 0, :], nat[:, :], ACT.Copy).then_inc(h_hi.sem, 1)

        def h_transposed(n):
            act.wait_ge(h_tp.sem, h_tp.at(n))
            act.wait_ge(r_p.sem, r_p.at(n.shift(-1)))
            act.activation(hT[:, :, :, :].rearrange("p a c n -> p (a c) n"), half(md[0]), ACT.Copy).then_inc(h_T.sem, 1)

        def router_exp(n):
            act.wait_ge(r_gap.sem, r_gap.at(n))
            act.activation(gap[:, 1:2], gap[:, 0:1], ACT.Exp, scale=1 / WS).then_inc(r_ex.sem, 1)

        def step(b, c, d, n, m):
            for u in range(2 * GROUPS):
                exps(b, u)
                if u == 0:
                    if n:
                        ctx_hi(n)
                        mask_hi(n)
                    w_slice(b)
                if u == 1 and d:
                    out_hi(d)
                if u == 2 and n:
                    q_high(n)
                if u == 2 and c:
                    router_exp(c)
                if u == 3 and n:
                    ctx_turned(n)
                if u == 3 and d:
                    out_T(d)
                if u == 4 and n:
                    k_high(n)
                if u == 5 and d:
                    h_high(d)
                if u == 6 and n:
                    ak_high(n)
                if u == 7 and d:
                    h_transposed(d)
                if u == 11 and m:
                    x_high(m)
                if u >= 8 and n:
                    stack_out(n, u - 8)
            if n:
                own_values(n)
                adapter_values(n)
            if m:
                x_turned(m)

        def first(n):
            mask_hi(n)
            x_turned(n)
            ctx_hi(n)
            q_high(n)
            ctx_turned(n)
            k_high(n)
            ak_high(n)
            x_high(n.shift(1))
            for g in range(GROUPS):
                stack_out(n, g)
            own_values(n)
            adapter_values(n)
            x_turned(n.shift(1))

        def last(n):
            router_exp(n.shift(-1))
            out_hi(n)
            out_T(n)
            h_high(n)
            h_transposed(n)
            router_exp(n)

        walk(act, step, first, last)

    @block.vector
    def _(dve):
        def ctx_lo(n):
            dve.wait_ge(c_hi.sem, c_hi.at(n))
            dve.tensor_tensor(xcs[:, 1, :], cin[:, :], xcs[:, 0, :], ALU.subtract).then_inc(c_lo.sem, 1)

        def mask_lo(n):
            dve.wait_ge(m_hi.sem, m_hi.at(n))
            dve.tensor_tensor(mskp[:, n.par, 1, :], msk[:, n.par, :], mskp[:, n.par, 0, :].bitcast(F32),
                              ALU.subtract).then_inc(m_lo.sem, 1)

        def x_low(n):
            dve.wait_ge(x_hi.sem, x_hi.at(n))
            dve.tensor_tensor(xcs[:, 1, :], nat[:, :], xcs[:, 0, :], ALU.subtract).then_inc(x_lo.sem, 1)

        def stats_x(n):
            dve.wait_ge(x_in.sem(n), x_in.at(n))
            dve.bn_stats(stat[:, 0, 0:6], xin[:, n.par, :]).then_inc(x_part.sem, 1)
            dve.wait_ge(x_part.sem, x_part.at(n, 1))
            dve.memset(held[:, 0:1], 0.0)
            dve.bn_aggr(mv[:, 0, 0:2], stat[:, 0, 0:6]).then_inc(x_part.sem, 1)
            dve.wait_ge(x_part.sem, x_part.at(n, 2))
            dve.tensor_scalar(mv[:, 0, 2:3], mv[:, 0, 1:2], EPS, None, ALU.add).then_inc(x_ve.sem, 1)

        def norm_x(n):
            dve.wait_ge(x_rs.sem, x_rs.at(n))
            dve.wait_ge(h_hi.sem, h_hi.at(n.shift(-3)))
            dve.wait_ge(h_lo.sem, h_lo.at(n.shift(-3)))
            dve.tensor_scalar(nat[:, :], xin[:, n.par, :], mv[:, 0, 0:1], mv[:, 0, 3:4], ALU.subtract,
                              ALU.mult).then_inc(x_n.sem, 1)

        pool_c_all = 20
        dve.wait_ge(pool_c.sem, pool_c_all)
        dve.tensor_copy(ident16[:, :], identf[:, :]).then_inc(dve_c.sem, 1)
        dve.tensor_copy(identr[:, :], identf[:, :]).then_inc(dve_c.sem, 1)
        dve.tensor_copy(ident_bf[:, :], identf[:, :]).then_inc(dve_c.sem, 1)
        for k, n in enumerate((0, 1, 2, 3)):
            if k == 0:
                stats_x(A0)
                norm_x(A0)
            if k == 1:
                x_low(A0)
                mask_lo(A0)
            dve.wait_ge(wt_hi.sem, k + 1)
            dve.scalar_tensor_tensor(out=wts[n][:, :, 1, :], in0=keep["stage"](n), scalar=WS,
                                     in1=wts[n][:, :, 0, :], op0=ALU.mult, op1=ALU.subtract).then_inc(wt_lo.sem, 1)
        dve.wait_ge(act_c.sem, 2)
        dve.scalar_tensor_tensor(out=rw[:, :, 1, :], in0=rwf[:, :, :], scalar=WS, in1=rw[:, :, 0, :],
                                 op0=ALU.mult, op1=ALU.subtract).then_inc(dve_c.sem, 1)
        dve.wait_ge(const_in.sem(A0), const_in.at(A0.shift(2)))

        def ak_low(n):
            dve.wait_ge(ak_hi.sem, ak_hi.at(n))
            for j in range(2):
                i = dve.scalar_tensor_tensor(out=aks[:, :, 2 * j + 1, :], in0=heads(ma[1]), scalar=1 / WS,
                                             in1=aks[:, :, 0, :], op0=ALU.mult, op1=ALU.subtract)
            i.then_inc(ak_lo.sem, 1)

        def rotate(n, tab, bank, proj, e1, e2, free):
            dve.wait_ge(proj.sem, proj.at(n))
            free()
            cos = rope[:, tab, :].unsqueeze(1).to_broadcast([P, NH, HD])
            dve.tensor_tensor(heads(t1), heads(bank), cos, ALU.mult).then_inc(e1.sem, 1)
            for j in range(2):
                a, z = slice(8 * j, 8 * j + 8), slice(8 - 8 * j, 16 - 8 * j)
                sin = rope[:, tab + 1, a].unsqueeze(1).to_broadcast([P, NH, HD // 2])
                i = dve.tensor_tensor(heads(t2)[:, :, a], heads(bank)[:, :, z], sin, ALU.mult)
            i.then_inc(e2.sem, 1)

        def rotate_q(n):
            def free():
                dve.wait_ge(k_lo.sem, k_lo.at(n.shift(-1)))
                dve.wait_ge(k_hi.sem, k_hi.at(n.shift(-1)))
            rotate(n, 0, ma[0], q_p, q_t1, q_t2, free)

        def rotate_k(n):
            def free():
                dve.wait_ge(q_lo.sem, q_lo.at(n))
                dve.wait_ge(q_hi.sem, q_hi.at(n))
            rotate(n, 2, ma[1], k_p, k_t1, k_t2, free)

        def maxima(n, g):
            dve.wait_ge(s_pe.sem, s_pe.at(n, g + 1))
            dve.wait_ge(s_own.sem, s_own.at(n, g))
            dve.tensor_reduce(mx[:, 1, 4 * g:4 * g + 4], sm[1][:, :, :], AX.X, ALU.max).then_inc(s_ad.sem, 1)
            for j in range(4):
                h = 4 * g + j
                i = dve.tensor_tensor_reduce(sm[0][:, j, :], sm[0][:, j, :], msk[:, n.par, :], 1.0, -3.4028235e38,
                                             ALU.add, ALU.max, mx[:, 0, h:h + 1])
            i.then_inc(s_own.sem, 1)

        def neg_max(n):
            dve.wait_ge(s_own.sem, s_own.at(n))
            dve.wait_ge(s_ad.sem, s_ad.at(n))
            dve.wait_ge(mp_t.sem, mp_t.at(n.shift(-1)))
            p3 = [mp[:, :, k, :] for k in range(3)]
            dve.tensor_scalar(p3[0], mx[:, :, :], -1.0, None, ALU.mult).then_inc(m_part.sem, 1)
            dve.wait_ge(m_part.sem, m_part.at(n, 1))
            dve.scalar_tensor_tensor(out=mr[:, :, :], in0=mx[:, :, :], scalar=-1.0, in1=p3[0],
                                     op0=ALU.mult, op1=ALU.subtract).then_inc(m_part.sem, 1)
            dve.wait_ge(m_part.sem, m_part.at(n, 2))
            dve.tensor_copy(p3[1], mr[:, :, :]).then_inc(m_part.sem, 1)
            dve.wait_ge(m_part.sem, m_part.at(n, 3))
            dve.tensor_tensor(mr[:, :, :], mr[:, :, :], p3[1], ALU.subtract).then_inc(m_part.sem, 1)
            dve.wait_ge(m_part.sem, m_part.at(n, 4))
            dve.tensor_copy(p3[2], mr[:, :, :]).then_inc(mp3.sem, 1)
            dve.wait_ge(mp_t.sem, mp_t.at(n))
            dve.tensor_copy(mT[:, :, :], m_bank()[0:3 * NH]).then_inc(m_T.sem, 1)

        def values_out(n, o):
            dve.wait_ge(av_pe.sem, av_pe.at(n, 4 * o + 4))
            if o == 0:
                dve.wait_ge(n_o.sem, n_o.at(n.shift(-1)))
            dve.tensor_copy(avs[:, 8 * o:8 * o + 8, :, :], av[o % 2][:, :, :, :]).then_inc(av_s.sem, 1)

        def norm_out(n):
            dve.wait_ge(av_s.sem, av_s.at(n))
            dve.reciprocal(rc[:, :, :], avs[:, :, :, HD]).then_inc(n_rc.sem, 1)
            dve.wait_ge(n_rc.sem, n_rc.at(n))
            dve.tensor_tensor(rc[:, :, 1], rc[:, :, 1], tg[:, :], ALU.mult).then_inc(n_rg.sem, 1)
            dve.wait_ge(n_rg.sem, n_rg.at(n))
            dve.tensor_tensor(avs[:, :, 1, 0:HD], avs[:, :, 1, 0:HD],
                              rc[:, :, 1:2].to_broadcast([P, NH, HD]), ALU.mult).then_inc(n_o2.sem, 1)

        def sum_out(n, x_batch):
            if x_batch:
                dve.wait_ge(x_hi.sem, x_hi.at(x_batch))
                dve.wait_ge(x_lo.sem, x_lo.at(x_batch))
            dve.wait_ge(n_o1.sem, n_o1.at(n))
            dve.wait_ge(n_o2.sem, n_o2.at(n))
            dve.wait_ge(h_hi.sem, h_hi.at(n.shift(-1)))
            dve.wait_ge(h_lo.sem, h_lo.at(n.shift(-1)))
            dve.tensor_tensor(heads(nat), avs[:, :, 0, 0:HD], avs[:, :, 1, 0:HD], ALU.add).then_inc(n_o.sem, 1)

        def out_low(n):
            dve.wait_ge(o_hi.sem, o_hi.at(n))
            dve.tensor_tensor(ohs[:, 1, :], nat[:, :], ohs[:, 0, :], ALU.subtract).then_inc(o_lo.sem, 1)

        def residual(n):
            dve.wait_ge(o_p.sem, o_p.at(n))
            dve.wait_ge(x_kept.sem, x_kept.at(n))
            dve.wait_ge(out_st.sem(n.shift(-1)), out_st.at(n.shift(-1)))
            dve.scalar_tensor_tensor(out=x2[:, :], in0=md[1][:, :], scalar=1 / WS, in1=xres[:, n.par, :],
                                     op0=ALU.mult, op1=ALU.add).then_inc(x_2.sem, 1)
            dve.wait_ge(x_2.sem, x_2.at(n))
            dve.bn_stats(stat[:, 1, 0:6], x2[:, :]).then_inc(h_part.sem, 1)
            dve.wait_ge(h_part.sem, h_part.at(n, 1))
            dve.memset(held[:, 0:1], 0.0)
            dve.bn_aggr(mv[:, 1, 0:2], stat[:, 1, 0:6]).then_inc(h_part.sem, 1)
            dve.wait_ge(h_part.sem, h_part.at(n, 2))
            dve.tensor_scalar(mv[:, 1, 2:3], mv[:, 1, 1:2], EPS, None, ALU.add).then_inc(h_ve.sem, 1)

        def norm_h(n):
            dve.wait_ge(h_rs.sem, h_rs.at(n))
            dve.wait_ge(o_hi.sem, o_hi.at(n))
            dve.wait_ge(o_lo.sem, o_lo.at(n))
            dve.tensor_scalar(nat[:, :], x2[:, :], mv[:, 1, 0:1], mv[:, 1, 3:4], ALU.subtract,
                              ALU.mult).then_inc(h_n.sem, 1)

        def h_low(n):
            dve.wait_ge(h_hi.sem, h_hi.at(n))
            dve.tensor_tensor(ohs[:, 1, :], nat[:, :], ohs[:, 0, :], ALU.subtract).then_inc(h_lo.sem, 1)

        def router_logits(n):
            dve.wait_ge(r_p.sem, r_p.at(n))
            dve.tensor_copy(lg[:, :], md[1][:, 0:NE]).then_inc(r_lg.sem, 1)

        def router_top(n):
            dve.wait_ge(r_lg.sem, r_lg.at(n))
            dve.memset(held[:, 0:1], 0.0)
            dve.max(top[:, :], lg[:, :]).then_inc(r_pick.sem, 1)
            dve.wait_ge(r_pick.sem, r_pick.at(n, 1))
            dve.tensor_tensor(gap[:, 0:1], top[:, 1:2], top[:, 0:1], ALU.subtract).then_inc(r_gap.sem, 1)
            for k in range(2):
                dve.tensor_scalar(key[:, k, :], lg[:, :], top[:, k:k + 1], -float(NE), ALU.is_equal,
                                  ALU.mult).then_inc(r_pick.sem, 1)
                dve.wait_ge(r_pick.sem, r_pick.at(n, 2 + 4 * k))
                dve.tensor_tensor(key[:, k, :], key[:, k, :], iota8[:, :], ALU.add).then_inc(r_pick.sem, 1)
                dve.wait_ge(r_pick.sem, r_pick.at(n, 3 + 4 * k))
                if k:
                    dve.scalar_tensor_tensor(out=key[:, k, :], in0=oh[:, 0, :], scalar=2.0 * NE,
                                             in1=key[:, k, :], op0=ALU.mult, op1=ALU.add).then_inc(r_pick.sem, 1)
                    dve.wait_ge(r_pick.sem, r_pick.at(n, 8))
                dve.tensor_reduce(lowest[:, k:k + 1], key[:, k, :], AX.X, ALU.min).then_inc(r_pick.sem, 1)
                dve.wait_ge(r_pick.sem, r_pick.at(n, 4 + 5 * k))
                dve.tensor_scalar(oh[:, k, :], iota8[:, :], -float(NE), lowest[:, k:k + 1], ALU.add,
                                  ALU.is_equal).then_inc(r_pick.sem, 1)
                dve.wait_ge(r_pick.sem, r_pick.at(n, 5 + 5 * k))
            dve.wait_ge(f_p.sem, f_p.at(n.shift(-1)))
            dve.tensor_tensor(sel[:, :], oh[:, 0, :], oh[:, 1, :], ALU.add).then_inc(r_sel.sem, 1)

        def router_counts(n):
            dve.wait_ge(f_p.sem, f_p.at(n))
            dve.tensor_tensor(pos[:, :], md[1][:, 0:NE], count[:, :], ALU.add).then_inc(f_c.sem, 1)
            dve.wait_ge(f_c.sem, f_c.at(n))
            dve.tensor_tensor(count[:, :], md[1][:, NE:2 * NE], count[:, :], ALU.add).then_inc(f_cnt.sem, 1)

        def router_weights(n):
            dve.wait_ge(r_ex.sem, r_ex.at(n))
            dve.tensor_scalar(gap[:, 2:3], gap[:, 1:2], 1.0, None, ALU.add).then_inc(r_weigh.sem, 1)
            dve.wait_ge(r_weigh.sem, r_weigh.at(n, 1))
            dve.reciprocal(gap[:, 3:4], gap[:, 2:3]).then_inc(r_weigh.sem, 1)
            dve.wait_ge(r_weigh.sem, r_weigh.at(n, 2))
            dve.tensor_tensor(w2nd[:, :], gap[:, 1:2], gap[:, 3:4], ALU.mult).then_inc(r_weigh.sem, 1)
            dve.tensor_scalar(wsel[:, :], oh[:, 0, :], gap[:, 3:4], None, ALU.mult).then_inc(r_weigh.sem, 1)
            dve.wait_ge(r_weigh.sem, r_weigh.at(n, 3))
            dve.wait_ge(r_weigh.sem, r_weigh.at(n, 4))
            dve.wait_ge(list_st.sem, list_st.at(n.shift(-1)))
            dve.tensor_copy(row[:, :, :].bitcast(I32)[:, :, 0], tok[:, 0:1].to_broadcast([P, NE]))
            dve.scalar_tensor_tensor(out=row[:, :, 1], in0=oh[:, 1, :], scalar=w2nd[:, :], in1=wsel[:, :],
                                     op0=ALU.mult, op1=ALU.add).then_inc(r_row.sem, 1)
            dve.tensor_scalar(unsel[:, :], sel[:, :], -1.0, 1.0, ALU.mult, ALU.add).then_inc(r_un.sem, 1)
            dve.wait_ge(r_un.sem, r_un.at(n))
            dve.scalar_tensor_tensor(out=pos[:, :], in0=unsel[:, :], scalar=tok[:, 1:2], in1=pos[:, :],
                                     op0=ALU.mult, op1=ALU.add).then_inc(f_step.sem, 1)
            dve.wait_ge(f_step.sem, f_step.at(n, 1))
            dve.tensor_tensor(pos[:, :], pos[:, :], ebase[:, :], ALU.add).then_inc(f_step.sem, 1)
            dve.wait_ge(f_step.sem, f_step.at(n, 2))
            dve.tensor_copy(posi[:, :], pos[:, :]).then_inc(f_pos.sem, 1)
            dve.tensor_tensor(key[:, :, :], oh[:, :, :], pos[:, :].unsqueeze(1).to_broadcast([P, 2, NE]),
                              ALU.mult).then_inc(f_step.sem, 1)
            dve.wait_ge(f_step.sem, f_step.at(n, 3))
            dve.tensor_reduce(entry[:, bass.ds(n.n, 1), :].rearrange("p a k -> p (a k)"), key[:, :, :], AX.X,
                              ALU.add)
            dve.tensor_scalar(tok[:, 0:1], tok[:, 0:1], float(P), None, ALU.add)
            dve.tensor_scalar(tok[:, 1:2], tok[:, 1:2], float(-P), None, ALU.add).then_inc(f_step.sem, 1)
            dve.wait_ge(f_step.sem, f_step.at(n, 4))

        def step(b, c, d, n, m):
            if d:
                norm_out(d)
                sum_out(d, n)
            if n:
                ctx_lo(n)
                mask_lo(n)
            if d:
                out_low(d)
            if n:
                rotate_q(n)
            if c:
                router_top(c)
                router_counts(c)
            if n:
                rotate_k(n)
            if c:
                router_weights(c)
            values_out(b, 0)
            if d:
                residual(d)
                norm_h(d)
                h_low(d)
            if n:
                ak_low(n)
            values_out(b, 1)
            if d:
                router_logits(d)
            if m:
                stats_x(m)
            if n:
                maxima(n, 0)
            if m:
                norm_x(m)
            if n:
                maxima(n, 1)
                maxima(n, 2)
            values_out(b, 2)
            if n:
                for g in range(3, 7):
                    maxima(n, g)
            values_out(b, 3)
            if n:
                maxima(n, 7)
                neg_max(n)

        def first(n):
            rotate_q(n)
            ctx_lo(n)
            rotate_k(n)
            ak_low(n)
            stats_x(n.shift(1))
            norm_x(n.shift(1))
            for g in range(GROUPS):
                maxima(n, g)
            neg_max(n)

        def last(n):
            norm_out(n)
            sum_out(n, None)
            router_top(n.shift(-1))
            out_low(n)
            router_counts(n.shift(-1))
            router_weights(n.shift(-1))
            residual(n)
            norm_h(n)
            h_low(n)
            router_logits(n)
            router_top(n)
            router_counts(n)
            router_weights(n)
            experts_slots()

        def experts_slots():
            past = qs[:, :, :, :].rearrange("p h a n -> p (h a n)").bitcast(F32)[:, 0:SLOTS * NE]
            past2 = ks[:, :, :, :].rearrange("p h a n -> p (h a n)").bitcast(F32)[:, 0:SLOTS * NE]
            past, past2 = (t.rearrange("p (s e) -> p s e", e=NE) for t in (past, past2))
            steps = t1[:, 0:NE * (T // P)].rearrange("p (e k) -> p e k", e=NE)
            made = [0]
            dve.wait_ge(iot_d.sem, iot_d.at(Batch(0, 0)))

            def table(ins):
                ins.then_inc(tab.sem, 1)
                made[0] += 1
                dve.wait_ge(tab.sem, made[0])

            table(dve.tensor_copy(slot[:, :], iot[:, :]))
            table(dve.tensor_scalar(steps[:, 0, :], slot[:, 0:T // P], float(P), None, ALU.mult))
            table(dve.tensor_copy(steps[:, 1:NE, :], steps[:, 0:1, :].to_broadcast([P, NE - 1, T // P])))
            table(dve.tensor_tensor(steps[:, :, :], count[:, :].unsqueeze(2).to_broadcast([P, NE, T // P]),
                                    steps[:, :, :], ALU.is_gt))
            table(dve.tensor_reduce(tiles[:, :], steps[:, :, :], AX.X, ALU.add))
            table(dve.tensor_tensor_scan(ends[:, :], tiles[:, :], tiles[:, :], 0.0, ALU.add, ALU.bypass))
            table(dve.tensor_tensor(past[:, :, :], ends[:, :].unsqueeze(1).to_broadcast([P, SLOTS, NE]),
                                    slot[:, :].unsqueeze(2).to_broadcast([P, SLOTS, NE]), ALU.is_le))
            table(dve.tensor_tensor(past2[:, :, :], past[:, :, :],
                                    tiles[:, :].unsqueeze(1).to_broadcast([P, SLOTS, NE]), ALU.mult))
            table(dve.tensor_reduce(ex[:, :], past[:, :, :], AX.X, ALU.add))
            table(dve.tensor_reduce(begin[:, :], past2[:, :, :], AX.X, ALU.add))
            table(dve.tensor_scalar(valid[:, :], ex[:, :], float(NE), None, ALU.is_lt))
            table(dve.tensor_tensor(ex[:, :], ex[:, :], valid[:, :], ALU.mult))
            table(dve.tensor_tensor(at[:, :], slot[:, :], begin[:, :], ALU.subtract))
            table(dve.scalar_tensor_tensor(out=at[:, :], in0=ex[:, :], scalar=float(T // P), in1=at[:, :],
                                           op0=ALU.mult, op1=ALU.add))
            table(dve.tensor_copy(exi[:, :], ex[:, :]))
            table(dve.tensor_tensor(ati[:, :], at[:, :], valid[:, :], ALU.mult))
            assert made[0] == TAB

        walk(dve, step, first, last)

    @block.tensor
    def _(pe):
        def transposes(bank, src):
            for part in range(2):
                for c in range(NC_):
                    i = pe.transpose(half(bank)[:, part * NC_ + c, :], src[:, part, c * P:(c + 1) * P], ident16[:, :])
            return i

        def project(bank, xt, w, cols=D):
            for n in range(len(TERMS) * NC_):
                (a, z), c = TERMS[n // NC_], n % NC_
                i = pe.matmul(bank[:, 0:cols], xt[:, a, c, :], w[:, c, z, :], start=(n == 0), stop=(n == 11))
            return i

        def wait_weight(k):
            pe.wait_ge(wt_lo.sem, k)

        def x_turn(n):
            pe.wait_ge(x_hi.sem, x_hi.at(n))
            pe.wait_ge(x_lo.sem, x_lo.at(n))
            pe.wait_ge(v_v.sem, v_v.at(n.shift(-1)))
            transposes(ma[0], xcs).then_inc(x_tp.sem, 1)

        def q(n):
            pe.wait_ge(x_T.sem, x_T.at(n))
            project(ma[0], xT, wq).then_inc(q_p.sem, 1)

        def k(n):
            pe.wait_ge(av_v.sem, av_v.at(n.shift(-1)))
            project(ma[1], xT, wk).then_inc(k_p.sem, 1)

        def ctx_turn(n):
            pe.wait_ge(c_hi.sem, c_hi.at(n))
            pe.wait_ge(c_lo.sem, c_lo.at(n))
            pe.wait_ge(q_t1.sem, q_t1.at(n))
            pe.wait_ge(q_t2.sem, q_t2.at(n))
            transposes(ma[0], xcs).then_inc(c_tp.sem, 1)

        def ak(n):
            pe.wait_ge(c_T.sem, c_T.at(n))
            pe.wait_ge(k_t1.sem, k_t1.at(n))
            pe.wait_ge(k_t2.sem, k_t2.at(n))
            project(ma[1], cT, wk).then_inc(ak_p.sem, 1)

        def v(n):
            pe.wait_ge(stk_o.sem, stk_o.at(n, GROUPS - 1))
            project(ma[0], xT, wv).then_inc(v_p.sem, 1)

        def avp(n):
            pe.wait_ge(stk_o.sem, stk_o.at(n))
            project(ma[1], cT, wv).then_inc(av_p.sem, 1)

        def turn_pairs(src, bank, at, p0, count):
            for p in range(count):
                pair = src[:, 2 * (p0 + p):2 * (p0 + p) + 2, :, :].rearrange("q h a d -> q (h a d)")
                i = pe.transpose(half(bank)[:, at + p, :], pair, ident16[:, :])
            return i

        def stack(n, g):
            if g == 0:
                pe.wait_ge(q_lo.sem, q_lo.at(n))
                pe.wait_ge(k_lo.sem, k_lo.at(n))
                pe.wait_ge(ak_lo.sem, ak_lo.at(n))
            if g >= 2:
                pe.wait_ge(stk_o.sem, stk_o.at(n, g - 1))
            turn_pairs(qs, ma[g % 2], 0, 2 * g, 2)
            turn_pairs(ks, ma[g % 2], 2, 2 * g, 2)
            turn_pairs(aks, ma[g % 2], 4, 2 * g, 2).then_inc(stk_t.sem, 1)

        def scores(n, g):
            pe.wait_ge(stk_o.sem, stk_o.at(n, g + 1))
            if g == 0:
                pe.wait_ge(r_lg.sem, r_lg.at(n.shift(-2)))
            for path, keys, used in ((1, akst, s_ad), (0, kst, s_own)):
                pe.wait_ge(used.sem, used.at(n, g))
                for j in range(4):
                    h = 4 * g + j
                    i = pe.matmul(sm[path][:, j, :], qz[:, h // 2, h % 2, :], keys[:, h // 2, :],
                                  start=True, stop=True)
            i.then_inc(s_pe.sem, 1)

        def max_turn(n):
            pe.wait_ge(mp3.sem, mp3.at(n))
            for path in range(2):
                i = pe.transpose(m_bank()[0:3 * NH, path, :], mp[:, path, :, :].rearrange("p a h -> p (a h)"),
                                 ident_bf[:, :])
            i.then_inc(mp_t.sem, 1)

        def scores_T(n, u):
            g, path = u // 2, u % 2
            if u == 0:
                pe.wait_ge(m_T.sem, m_T.at(n))
                pe.wait_ge(m_lo.sem, m_lo.at(n))
                pe.wait_ge(m_hi.sem, m_hi.at(n))
            if u >= 2:
                pe.wait_ge(p_ex.sem, p_ex.at(n, u - 1))
            bank, keys = st[path], (kst, akst)[path]
            for j in range(2):
                p = 2 * g + j
                pe.matmul(bank[:, 2 * j:2 * j + 2, :], keys[:, p, :], qz[:, p, :, :], start=(j == 0), stop=False,
                          skip_group_check=True)
            if path == 0:
                for part in range(2):
                    pe.matmul(bank[:, :, :], mskp[:, n.par, part, :],
                              identr[:, :].unsqueeze(1).to_broadcast([P, 4, P]), start=False, stop=False,
                              skip_group_check=True)
            for j in range(4):
                h = 4 * g + j
                i = pe.matmul(bank[:, j, :], hsel[:, h:h + 1].to_broadcast([3 * NH, P]), mT[:, path, :],
                              start=False, stop=(j == 3), skip_group_check=True)
            i.then_inc(t_pe.sem, 1)

        def values(n, u):
            g, path = u // 2, u % 2
            pe.wait_ge(p_ex.sem, p_ex.at(n, u + 1))
            if u == 0:
                pe.wait_ge(av_v.sem, av_v.at(n))
                pe.wait_ge(v_v.sem, v_v.at(n))
            if u % 4 == 0:
                pe.wait_ge(av_s.sem, av_s.at(n, u // 4 - 1))
            for j in range(4):
                h = 4 * g + j
                i = pe.matmul(av[g // 2 % 2][:, h % 8, path, :], pr[:, path, j, :], vv[:, n.par, path, h, :],
                              start=True, stop=True)
            i.then_inc(av_pe.sem, 1)

        def out_turn(n):
            pe.wait_ge(o_hi.sem, o_hi.at(n))
            pe.wait_ge(o_lo.sem, o_lo.at(n))
            transposes(md[0], ohs).then_inc(o_tp.sem, 1)

        def out_project(n):
            pe.wait_ge(o_T.sem, o_T.at(n))
            pe.wait_ge(f_cnt.sem, f_cnt.at(n.shift(-1)))
            pe.wait_ge(f_c.sem, f_c.at(n.shift(-1)))
            project(md[1], oT, wo).then_inc(o_p.sem, 1)

        def h_turn(n):
            pe.wait_ge(h_lo.sem, h_lo.at(n))
            pe.wait_ge(h_hi.sem, h_hi.at(n))
            transposes(md[0], ohs).then_inc(h_tp.sem, 1)

        def router(n):
            pe.wait_ge(h_T.sem, h_T.at(n))
            project(md[1], hT, rw, NE).then_inc(r_p.sem, 1)

        def places(n):
            pe.wait_ge(r_sel.sem, r_sel.at(n))
            pe.matmul(md[1][:, 0:NE], tri[:, :], sel[:, :], start=True, stop=True)
            pe.matmul(md[1][:, NE:2 * NE], ones[:, :], sel[:, :], start=True, stop=True).then_inc(f_p.sem, 1)

        def step(b, c, d, n, m):
            for u in range(2 * GROUPS):
                scores_T(b, u)
                if u == 1 and n:
                    q(n)
                if u == 2 and n:
                    k(n)
                    ctx_turn(n)
                if u == 2 and d:
                    out_turn(d)
                if u == 3 and c:
                    places(c)
                if u == 4 and d:
                    out_project(d)
                if u == 5 and n:
                    ak(n)
                if u == 7 and d:
                    h_turn(d)
                if u == 8 and d:
                    router(d)
                if u >= 8 and n:
                    stack(n, u - 8)
                if u >= 9 and n:
                    scores(n, u - 9)
                if u:
                    values(b, u - 1)
            values(b, 2 * GROUPS - 1)
            if n:
                scores(n, GROUPS - 1)
                v(n)
                avp(n)
            if m:
                x_turn(m)
            if n:
                max_turn(n)

        def first(n):
            pe.wait_ge(dve_c.sem, 1)
            x_turn(n)
            wait_weight(1)
            q(n)
            wait_weight(2)
            k(n)
            ctx_turn(n)
            ak(n)
            stack(n, 0)
            for g in range(GROUPS):
                if g + 1 < GROUPS:
                    stack(n, g + 1)
                scores(n, g)
            wait_weight(4)
            pe.wait_ge(dve_c.sem, 4)
            v(n)
            avp(n)
            x_turn(n.shift(1))
            max_turn(n)

        def last(n):
            places(n.shift(-1))
            out_turn(n)
            out_project(n)
            h_turn(n)
            router(n)
            places(n)

        walk(pe, step, first, last)


def expert_phase(nc, ctx, dram, keep):
    def sb(name, shape, dt):
        return ctx.enter_context(nc.sbuf_tensor(name, shape, dt))

    def ps(name, shape, dt):
        return ctx.enter_context(nc.psum_tensor(name, shape, dt))

    def sem(name):
        return keep["semaphores"].enter_context(nc.semaphore(name))

    def ev(name, per=1):
        return Event(sem(name), per)

    w1s, count, ident16, held = keep["w1s"], keep["count"], keep["ident16"], keep["held"]
    entry, tab = keep["entry"], keep["tab"]
    iot, slot, tiles, ends, ex, begin, valid, at, exi, ati = keep["slots"]
    KF = len(FCH)

    w2f = keep["w2f"] + [sb("w2f3", [P, KF, D], F32)]
    w2s = sb("w2s", [P, NE, KF, 2, D], F16)
    lrow = sb("lrow", [P, LB, 2], F32)
    wrow = sb("wrow", [P, 2], F32)
    hg = sb("hg", [P, 2, 2, D], F16)
    hgT = sb("hgT", [P, 2, 2, NC_, P], F16)
    sg = sb("sg", [P, F], F32)
    ya = sb("ya", [P, F], F32)
    yp = sb("yp", [P, 2, F], F16)
    yT = sb("yT", [P, 2, KF, P], F16)
    yo = [sb(f"yo{k}", [P, D], F32) for k in range(LB)]
    last_of = sb("last_of", [P, NE - 1], F32)
    shift = sb("shift", [P, NE - 1], F32)
    beyond = yo[0][:, 0:2 * NB * (NE - 1)].rearrange("p (b e) -> p b e", e=NE - 1)
    moved = sb("moved", [P, 2 * NB], F32)
    res_row = sb("res_row", [P, 2 * NB], I32)
    idx = sb("idx", [P, LB, 2], I32)
    x2_kept = sb("x2_kept", [P, NB // LB, D], F32)
    res, x2 = [t[:, 0:2, :] for t in w2f], [t[:, 2, :] for t in w2f]

    y1 = [[ps(f"y1_{k}{j}", [P, 512], F32) for j in range(2)] for k in range(2)]
    px = ps("px", [P, 8, P], F16)
    py = ps("py", [P, 8, P], F16)
    y2 = [ps(f"y2_{k}", [P, 512], F32) for k in range(2)]

    w2_in = keep["w2_in"]
    w2_hi, w2_lo = ev("w2_hi"), ev("w2_lo")
    l_in = Loaded([sem(f"l_in{k}") for k in range(LB)])
    g_in = Loaded([sem(f"g_in{k}") for k in range(LB)])
    y_st = Loaded([sem(f"y_st{k}") for k in range(LB)])
    gather_held = ev("gather_held")
    kept_in = ev("kept_in", 16)
    x2_in, o_st = (Loaded([sem(f"{n}{k}") for k in range(LB)]) for n in ("x2_in", "o_st"))
    res_in = [Event(sem(f"res_in{k}"), 32) for k in range(LB)]
    i_cp, res_held, sum_1, sum_2 = ev("i_cp"), ev("res_held"), ev("sum_1"), ev("sum_2")
    w_row, g_tp, g_T, gate_p, up_p, g_silu, y_a, y_hi, y_lo, y_tp, y_T, y_p, y_o = (
        ev(n) for n in ("w_row", "g_tp", "g_T", "gate_p", "up_p", "g_silu", "y_a", "y_hi", "y_lo", "y_tp",
                        "y_T", "y_p", "y_o"))
    block = ctx.enter_context(nc.Block())

    def number(eng, table, n, top):
        return eng.value_load(table[0:1, bass.ds(n.n, 1)], min_val=0, max_val=top)

    def walk(eng, step):
        head = (SLOTS - 1) % LB + LB
        for k in range(head):
            step(Batch(0, k, LB), k == 0, False)
        with eng.Fori(0, (SLOTS - 1 - head) // LB) as it:
            for k in range(LB):
                step(Batch(it, head + k, LB), False, False)
        step(Batch(0, SLOTS - 1, LB), False, True)

    AHEAD = LB - 1

    def walk_tokens(eng, ready, step):
        for k in range(AHEAD):
            ready(Batch(0, k, LB))
        for k in range(LB):
            ready(Batch(0, k + AHEAD, LB))
            step(Batch(0, k, LB))
        with eng.Fori(0, NB // LB - 2) as it:
            for k in range(LB, 2 * LB):
                ready(Batch(it, k + AHEAD, LB))
                step(Batch(it, k, LB))
        for k in range(NB - LB, NB):
            if k + AHEAD < NB:
                ready(Batch(0, k + AHEAD, LB))
            step(Batch(0, k, LB))

    @block.sync
    def _(sp):
        def load_w2(e):
            sp.dma_start(w2f[e % LB][:, 0:2, :], dram["w2a"][e]).then_inc(w2_in[e % LB], 16)
            sp.dma_start(w2f[e % LB][0:96, 2, :], dram["w2b"][e]).then_inc(w2_in[e % LB], 16)

        def load_last_w2():
            for e in range(LB, NE):
                sp.wait_ge(w2_hi.sem, w2_hi.at(Batch(0, 0), 2 * (e - LB) + 2))
                sp.wait_ge(w2_lo.sem, w2_lo.at(Batch(0, 0), 2 * (e - LB) + 2))
                load_w2(e)

        load_w2(LB - 1)
        sp.wait_ge(tab.sem, tab.at(Batch(0, 0), TAB))

        def store(s):
            target = dram["y_tile"](s)
            sp.wait_ge(y_o.sem, y_o.at(s))
            sp.dma_start(target, yo[s.off % LB][:, :]).then_inc(y_st.sem(s), 16)

        def step(s, is_first, is_last):
            place = number(sp, ati, s, NE * (T // P) - 1)
            source = dram["list_tiles"][bass.ds(place, 1), :, :].rearrange("a p n -> (a p) n")
            sp.wait_ge(w_row.sem, w_row.at(s.shift(-LB)))
            sp.wait_ge(g_in.sem(s), g_in.at(s.shift(-LB)))
            sp.dma_start(lrow[:, s.off % LB, :], source).then_inc(l_in.sem(s), 16)
            if isinstance(s.n, int) and s.n == 2:
                load_last_w2()
            for k in range(2):
                if isinstance(s.n, int) and s.n == LB + k:
                    some = slice(k * (NB // LB // 2), (k + 1) * (NB // LB // 2))
                    sp.dma_start(x2_kept[:, some, :], dram["kept"][:, some, :]).then_inc(kept_in.sem, 16)
            if s.off >= 3:
                store(s.shift(-3))
            if is_last:
                for k in (-2, -1, 0):
                    store(s.shift(k))

        walk(sp, step)

        def load_x2(n):
            if n.off % LB == 0:
                return
            source = dram["out"](n)
            sp.wait_ge(sum_1.sem, sum_1.at(n.shift(-LB)))
            sp.dma_start(x2[n.off % LB], source).then_inc(x2_in.sem(n), 16)

        def store_out(n):
            target = dram["out"](n)
            sp.wait_ge(sum_2.sem, sum_2.at(n))
            sp.dma_start(target, yo[n.off % LB][:, :]).then_inc(o_st.sem(n), 16)

        walk_tokens(sp, load_x2, store_out)
        for k in range(NB - LB, NB):
            sp.wait_ge(o_st.sem(Batch(0, k, LB)), o_st.at(Batch(0, k, LB)))

    @block.gpsimd
    def _(pool):
        def step(s, is_first, is_last):
            pool.wait_ge(l_in.sem(s), l_in.at(s))
            pool.wait_ge(g_tp.sem, g_tp.at(s.shift(-2)))
            pool.wait_ge(gather_held.sem, gather_held.at(s.shift(-1)))
            pool.tensor_tensor(held[:, 0:1], held[:, 2:3], held[:, 2:3], ALU.add).then_inc(gather_held.sem, 1)
            pool.indirect_dma_start(
                out=hg[:, s.par, :, :].rearrange("p a n -> p (a n)"), out_offset=None, in_=dram["h2_rows"],
                in_offset=bass.IndirectOffsetOnAxis(ap=lrow[:, s.off % LB, 0:1].bitcast(I32), axis=0)
            ).then_inc(g_in.sem(s), 16)

        walk(pool, step)
        for k in range(SLOTS - LB, SLOTS):
            pool.wait_ge(y_st.sem(Batch(0, k, LB)), y_st.at(Batch(0, k, LB)))

        def results(n):
            pool.wait_ge(i_cp.sem, i_cp.at(n))
            pool.wait_ge(sum_2.sem, sum_2.at(n.shift(-LB)))
            pool.wait_ge(res_held.sem, res_held.at(n.shift(-1)))
            pool.tensor_tensor(held[:, 1:2], held[:, 2:3], held[:, 2:3], ALU.add).then_inc(res_held.sem, 1)
            for j in range(2):
                pool.indirect_dma_start(
                    out=res[n.off % LB][:, j, :], out_offset=None, in_=dram["y_rows"],
                    in_offset=bass.IndirectOffsetOnAxis(ap=idx[:, n.off % LB, j:j + 1], axis=0)
                ).then_inc(res_in[n.off % LB].sem, 16)

        walk_tokens(pool, lambda n: None, results)

    @block.scalar
    def _(act):
        def rows_turned(s):
            act.wait_ge(g_tp.sem, g_tp.at(s))
            act.wait_ge(up_p.sem, up_p.at(s.shift(-2)))
            act.activation(hgT[:, s.par, :, :, :].rearrange("p a c n -> p (a c) n"), px[:, :, :],
                           ACT.Copy).then_inc(g_T.sem, 1)

        for e in range(NE):
            act.wait_ge(w2_in[e % LB], 32 * (e // LB) + 32)
            act.activation(w2s[:, e, 0:2, 0, :], w2f[e % LB][:, 0:2, :], ACT.Copy, scale=WS).then_inc(w2_hi.sem, 1)
            act.activation(w2s[0:96, e, 2, 0, :], w2f[e % LB][0:96, 2, :], ACT.Copy, scale=WS).then_inc(w2_hi.sem, 1)
            if e == LB - 1:
                rows_turned(Batch(0, 0, LB))

        def step(s, is_first, is_last):
            act.wait_ge(gate_p.sem, gate_p.at(s))
            act.wait_ge(y_a.sem, y_a.at(s.shift(-1)))
            act.activation(sg[:, :], y1[s.par][0][:, 0:F], ACT.Silu, scale=1 / WS).then_inc(g_silu.sem, 1)
            if not is_last:
                rows_turned(s.shift(1))
            act.wait_ge(y_a.sem, y_a.at(s))
            act.wait_ge(y_tp.sem, y_tp.at(s.shift(-1)))
            act.activation(yp[:, 0, :], ya[:, :], ACT.Copy).then_inc(y_hi.sem, 1)
            if not is_first:
                expert_out(s.shift(-1))
            if is_last:
                expert_out(s)

        def expert_out(s):
            act.wait_ge(y_p.sem, y_p.at(s))
            act.wait_ge(w_row.sem, w_row.at(s))
            act.wait_ge(y_st.sem(s), y_st.at(s.shift(-LB)))
            act.activation(yo[s.off % LB][:, :], y2[s.par][:, :], ACT.Copy, scale=wrow[:, s.par:s.par + 1]
                           ).then_inc(y_o.sem, 1)

        walk(act, step)

    @block.vector
    def _(dve):
        made = [TAB]

        def table(ins):
            ins.then_inc(tab.sem, 1)
            made[0] += 1
            dve.wait_ge(tab.sem, made[0])

        for e in range(NE):
            dve.wait_ge(w2_hi.sem, w2_hi.at(Batch(0, 0), 2 * e + 2))
            dve.scalar_tensor_tensor(out=w2s[:, e, 0:2, 1, :], in0=w2f[e % LB][:, 0:2, :], scalar=WS,
                                     in1=w2s[:, e, 0:2, 0, :], op0=ALU.mult, op1=ALU.subtract).then_inc(w2_lo.sem, 1)
            dve.scalar_tensor_tensor(out=w2s[0:96, e, 2, 1, :], in0=w2f[e % LB][0:96, 2, :], scalar=WS,
                                     in1=w2s[0:96, e, 2, 0, :], op0=ALU.mult, op1=ALU.subtract).then_inc(w2_lo.sem, 1)

        def result_rows():
            table(dve.tensor_scalar(last_of[:, :], slot[:, 1:NE], float(T), None, ALU.mult))
            table(dve.tensor_scalar(shift[:, :], tiles[:, 0:NE - 1], float(P), -float(T), ALU.mult, ALU.add))
            entries = entry[:, :, :].rearrange("p b k -> p (b k)")
            table(dve.tensor_tensor(beyond[:, :, :], entries.unsqueeze(2).to_broadcast([P, 2 * NB, NE - 1]),
                                    last_of[:, :].unsqueeze(1).to_broadcast([P, 2 * NB, NE - 1]), ALU.is_ge))
            table(dve.tensor_tensor(beyond[:, :, :], beyond[:, :, :],
                                    shift[:, :].unsqueeze(1).to_broadcast([P, 2 * NB, NE - 1]), ALU.mult))
            table(dve.tensor_reduce(moved[:, :], beyond[:, :, :], AX.X, ALU.add))
            table(dve.tensor_tensor(moved[:, :], moved[:, :], entries, ALU.add))
            table(dve.tensor_copy(res_row[:, :], moved[:, :]))

        def step(s, is_first, is_last):
            dve.wait_ge(l_in.sem(s), l_in.at(s))
            dve.wait_ge(y_o.sem, y_o.at(s.shift(-2)))
            dve.scalar_tensor_tensor(out=wrow[:, s.par:s.par + 1], in0=lrow[:, s.off % LB, 1:2],
                                     scalar=1 / (WS * YS), in1=valid[:, bass.ds(s.n, 1)],
                                     op0=ALU.mult, op1=ALU.mult).then_inc(w_row.sem, 1)
            dve.wait_ge(g_silu.sem, g_silu.at(s))
            dve.wait_ge(up_p.sem, up_p.at(s))
            dve.wait_ge(y_lo.sem, y_lo.at(s.shift(-1)))
            dve.wait_ge(y_hi.sem, y_hi.at(s.shift(-1)))
            dve.scalar_tensor_tensor(out=ya[:, :], in0=y1[s.par][1][:, 0:F], scalar=YS / WS, in1=sg[:, :],
                                     op0=ALU.mult, op1=ALU.mult).then_inc(y_a.sem, 1)
            dve.wait_ge(y_hi.sem, y_hi.at(s))
            dve.tensor_tensor(yp[:, 1, :], ya[:, :], yp[:, 0, :], ALU.subtract).then_inc(y_lo.sem, 1)
            dve.wait_ge(y_tp.sem, y_tp.at(s))
            dve.wait_ge(y_p.sem, y_p.at(s.shift(-1)))
            for part in range(2):
                dve.tensor_copy(yT[:, part, 0:2, :], py[:, KF * part:KF * part + 2, :])
                i = dve.tensor_copy(yT[0:96, part, 2, :], py[0:96, KF * part + 2, :])
            i.then_inc(y_T.sem, 1)
            if is_first:
                result_rows()

        walk(dve, step)

        def numbers(n):
            used = res_in[n.off % LB]
            dve.wait_ge(used.sem, 32 * n.use(LB))
            dve.tensor_copy(idx[:, n.off % LB, :], res_row[:, bass.ds(2 * n.n, 2)]).then_inc(i_cp.sem, 1)

        def add(n):
            if n.off % LB == 0:
                dve.wait_ge(kept_in.sem, kept_in.at(Batch(0, 1)))
                rows = x2_kept[:, bass.ds(n.use(LB), 1), :].rearrange("p a n -> p (a n)")
            else:
                dve.wait_ge(x2_in.sem(n), x2_in.at(n))
                rows = x2[n.off % LB]
            results = res_in[n.off % LB]
            dve.wait_ge(results.sem, 32 * n.use(LB) + 32)
            dve.wait_ge(o_st.sem(n), o_st.at(n.shift(-LB)))
            dve.tensor_tensor(yo[n.off % LB][:, :], rows, res[n.off % LB][:, 0, :],
                              ALU.add).then_inc(sum_1.sem, 1)
            dve.wait_ge(sum_1.sem, sum_1.at(n))
            dve.tensor_tensor(yo[n.off % LB][:, :], yo[n.off % LB][:, :], res[n.off % LB][:, 1, :],
                              ALU.add).then_inc(sum_2.sem, 1)

        walk_tokens(dve, numbers, add)

    @block.tensor
    def _(pe):
        def turn_rows(s):
            pe.wait_ge(g_in.sem(s), g_in.at(s))
            pe.wait_ge(g_T.sem, g_T.at(s.shift(-1)))
            for part in range(2):
                for c in range(NC_):
                    i = pe.transpose(px[:, part * NC_ + c, :], hg[:, s.par, part, c * P:(c + 1) * P], ident16[:, :])
            i.then_inc(g_tp.sem, 1)

        def inner(s, j, e):
            if j == 0:
                pe.wait_ge(g_T.sem, g_T.at(s))
            n = 0
            for a, z in TERMS:
                for c in range(NC_):
                    w = w1s[:, bass.ds(e * NC_ + c, 1), z, j * F:(j + 1) * F].rearrange("p a n -> p (a n)")
                    i = pe.matmul(y1[s.par][j][:, 0:F], hgT[:, s.par, a, c, :], w, start=(n == 0), stop=(n == 11))
                    n += 1
            i.then_inc((gate_p, up_p)[j].sem, 1)

        def turn_inner(s):
            pe.wait_ge(y_hi.sem, y_hi.at(s))
            pe.wait_ge(y_lo.sem, y_lo.at(s))
            for part in range(2):
                for k, (f0, fn) in enumerate(FCH):
                    i = pe.transpose(py[0:fn, KF * part + k, :], yp[:, part, f0:f0 + fn], ident16[:, :])
            i.then_inc(y_tp.sem, 1)

        def outer(s, e):
            pe.wait_ge(y_T.sem, y_T.at(s))
            pe.wait_ge(y_o.sem, y_o.at(s.shift(-2)))
            n = 0
            for a, z in TERMS:
                for k, (f0, fn) in enumerate(FCH):
                    w = w2s[0:fn, bass.ds(e, 1), k, z, :].rearrange("p a n -> p (a n)")
                    i = pe.matmul(y2[s.par][:, :], yT[0:fn, a, k, :], w, start=(n == 0), stop=(n == 8))
                    n += 1
            i.then_inc(y_p.sem, 1)

        pe.wait_ge(tab.sem, tab.at(Batch(0, 0), TAB))

        def step(s, is_first, is_last):
            d = s.shift(-1)
            if is_first:
                turn_rows(s)
            e = number(pe, exi, s, NE - 1)
            inner(s, 0, e)
            if not is_first:
                turn_inner(d)
            inner(s, 1, e)
            if not is_last:
                turn_rows(s.shift(1))
            if is_first:
                pe.wait_ge(w2_lo.sem, w2_lo.at(Batch(0, 0), 2 * NE))
                pe.wait_ge(w2_hi.sem, w2_hi.at(Batch(0, 0), 2 * NE))
            else:
                outer(d, number(pe, exi, d, NE - 1))
            if is_last:
                turn_inner(s)
                outer(s, number(pe, exi, s, NE - 1))

        walk(pe, step)


def program(nc, x, ctx, mask, wq, wk, wv, wo, gate, router, w1, w2a, w2b, rope, out):
    def tile(t):
        return lambda n: t[bass.ds(n.n, 1), :, :].rearrange("a p n -> (a p) n")

    h2 = nc.dram_tensor("h2_pairs", [T, 2 * D], F16, kind="Internal").ap()
    y = nc.dram_tensor("y", [SLOTS, P, D], F32, kind="Internal").ap()
    lists = nc.dram_tensor("lists", [NE * T, 2], F32, kind="Internal").ap()
    with ExitStack() as both:
        w1s = both.enter_context(nc.sbuf_tensor("w1s", [P, NE * NC_, 2, 2 * F], F16))
        count = both.enter_context(nc.sbuf_tensor("count", [P, NE], F32))
        ident16 = both.enter_context(nc.sbuf_tensor("ident16", [P, P], F16))
        qkv = [both.enter_context(nc.sbuf_tensor(f"w_{n}", [P, NC_, 2, D], F16)) for n in "qkv"]
        w2f = [t[:, :, :, :].rearrange("p c a n -> p (c a n)").bitcast(F32)[:, 0:len(FCH) * D].rearrange(
            "p (c n) -> p c n", n=D) for t in qkv]
        w2_in = [both.enter_context(nc.semaphore(f"w2_in{k}")) for k in range(4)]
        entry = both.enter_context(nc.sbuf_tensor("entry", [P, NB, 2], F32))
        slots, k = [], 0
        wst = both.enter_context(nc.sbuf_tensor("wst", [P, 2 * F], F32))
        for n, dt in ((SLOTS, I32), (SLOTS, F32), (NE, F32), (NE, F32), (SLOTS, F32), (SLOTS, F32),
                      (SLOTS, F32), (SLOTS, F32), (SLOTS, I32), (SLOTS, I32)):
            view = wst[:, k:k + n]
            slots.append(view.bitcast(I32) if dt == I32 else view)
            k += n
        assert k <= 2 * F
        tab = Event(both.enter_context(nc.semaphore("tab")))
        held = both.enter_context(nc.sbuf_tensor("held", [P, 4], F32))

        def stage(n):
            room = w1s[:, 20:32, :, :].rearrange("p s a n -> p (s a n)").bitcast(F32)
            return room[:, n * NC_ * D:(n + 1) * NC_ * D].rearrange("p (c n) -> p c n", c=NC_)

        keep = dict(w1s=w1s, count=count, ident16=ident16, stage=stage, held=held, entry=entry, semaphores=both,
                    qkv=qkv, w2f=w2f, w2_in=w2_in, slots=slots, wst=wst, tab=tab)
        with ExitStack() as stack:
            attention_phase(nc, stack, dict(
                x=tile(x), ctx=tile(ctx), mask=tile(mask), w=(wq, wk, wv, wo), gate=gate, router=router,
                w1=tile(w1), rope=rope, out=tile(out), h2=tile(h2.rearrange("(b p) n -> b p n", p=P)),
                lists=lists, w2a=w2a, w2b=w2b), keep)
        with ExitStack() as stack:
            expert_phase(nc, stack, dict(
                kept=out.rearrange("(j f) p n -> f p j n", f=LB)[0],
                w2a=w2a, w2b=w2b, h2_rows=h2, list_tiles=lists.rearrange("(t p) n -> t p n", p=P),
                y_tile=tile(y), y_rows=y.rearrange("s p n -> (s p) n"), out=tile(out)), keep)


def rope_tables():
    inv = 1.0 / 10000.0 ** (np.arange(0, HD, 2, dtype=np.float32) / HD)
    freqs = np.outer(np.arange(P, dtype=np.float32), inv)
    cos, sin = np.cos(freqs).astype(np.float32), np.sin(freqs).astype(np.float32)
    cos, sin = np.concatenate([cos, cos], 1), np.concatenate([-sin, sin], 1)
    q, k = np.float32(HD ** -0.5 / WS), np.float32(1 / WS)
    return np.stack([cos * q, sin * q, cos * k, sin * k], 1)


def kernel(x, ctx_2048, mask_Bx1xSxS_fk0, L0_xattn_Wq, L0_xattn_Wk, L0_xattn_Wv, L0_xattn_Wo, L0_xattn_gate,
           L0_ffn_router_w, L0_ffn_w1, L0_ffn_w2):
    import concourse.bacc as bacc
    from concourse.bass_utils import run_bass_kernel_spmd

    def chunks(w):
        return np.ascontiguousarray(np.asarray(w).reshape(NC_, P, -1).transpose(1, 0, 2))

    w1 = np.asarray(L0_ffn_w1).transpose(0, 2, 1).reshape(NE * NC_, P, 2 * F)
    w2 = np.asarray(L0_ffn_w2).transpose(0, 2, 1)
    arrays = {
        "x": np.asarray(x), "ctx": np.asarray(ctx_2048), "mask": np.asarray(mask_Bx1xSxS_fk0).reshape(NB, P, P),
        "wq": chunks(L0_xattn_Wq), "wk": chunks(L0_xattn_Wk), "wv": chunks(L0_xattn_Wv), "wo": chunks(L0_xattn_Wo),
        "gate": np.asarray(L0_xattn_gate).reshape(1, NH), "router": chunks(np.asarray(L0_ffn_router_w).T),
        "w1": w1, "w2a": w2[:, 0:2 * P].reshape(NE, 2, P, D).transpose(0, 2, 1, 3), "w2b": w2[:, 2 * P:],
        "rope": rope_tables(),
    }
    arrays = {f"in_{n}": np.ascontiguousarray(a) for n, a in arrays.items()}
    nc = bacc.Bacc("TRN2", target_bir_lowering=False, num_devices=1)
    args = [nc.dram_tensor(n, a.shape, mybir.dt.from_np(a.dtype), kind="ExternalInput").ap()
            for n, a in arrays.items()]
    out = nc.dram_tensor("out", (NB, P, D), F32, kind="ExternalOutput").ap()
    program(nc, *args, out)
    r = run_bass_kernel_spmd(nc, [arrays], core_ids=[0])
    return r.results[0]["out"]
```
